# Optimizing a Trainium2 kernel written in Bass

```python
import numpy as np
import jax
import jax.numpy as jnp

def _softmax(x, axis=-1):
    return jax.nn.softmax(x, axis=axis)

def _gelu(x):
    return jax.nn.gelu(x, approximate=True)

def _silu(x):
    return jax.nn.silu(x)

def _sigmoid(x):
    return jax.nn.sigmoid(x)

def _layernorm(x, axis=-1, eps=1e-05):
    m = jnp.mean(x, axis=axis, keepdims=True)
    v = jnp.var(x, axis=axis, keepdims=True)
    return (x - m) / jnp.sqrt(v + eps)

def _scatter_add(tgt, idx, src, axis=0):
    return tgt.at[idx].add(src)

def _segment_sum(src, seg, n):
    return jax.ops.segment_sum(src, seg, n)
kernel_name = 'mk_macaron_d1_jaxref_r8_800db0'

def setup_inputs(seed: int=0):
    np.random.seed(seed)
    _w = jnp.asarray

    def _L0_attn_setup():
        import math
        import jax, jax.numpy as jnp
        import numpy as np
        N_HEADS = 8
        EPS = 1e-05
        key = jax.random.key(seed)
        ks = jax.random.split(key, 5)
        B, L, D = (4, 256, 128)
        w_scale = 0.02
        return {'x': jax.random.normal(ks[0], (B, L, D), dtype=jnp.float32), 'Wq': jax.random.normal(ks[1], (D, D), dtype=jnp.float32) * w_scale, 'Wk': jax.random.normal(ks[2], (D, D), dtype=jnp.float32) * w_scale, 'Wv': jax.random.normal(ks[3], (D, D), dtype=jnp.float32) * w_scale, 'Wo': jax.random.normal(ks[4], (D, D), dtype=jnp.float32) * w_scale, 'gn_weight': jnp.ones((D,), dtype=jnp.float32), 'gn_bias': jnp.zeros((D,), dtype=jnp.float32)}
    _L0_attn_in = _L0_attn_setup()

    def _L0_ffn_setup():
        import jax, jax.numpy as jnp
        import numpy as np
        DIM = 128
        DEPTH = 6
        HEADS = 16
        DIM_HEAD = 64
        WINDOW = 32
        INNER = HEADS * DIM_HEAD
        DIM_INNER = int(DIM * 4 * 2 / 3)
        QK_SCALE = 8.0

        def shift_tokens(t):
            a, s = jnp.split(t, 2, -1)
            s = jnp.pad(s, ((0, 0), (1, 0), (0, 0)))[:, :-1]
            return jnp.concatenate([a, s], -1)

        def l2norm(t):
            return t / jnp.maximum(jnp.linalg.norm(t, axis=-1, keepdims=True), 1e-12)

        def rotate_half(x):
            x1, x2 = jnp.split(x, 2, -1)
            return jnp.concatenate([-x2, x1], -1)

        def rotary_tables(n):
            half = jnp.arange(0, DIM_HEAD, 2, dtype=jnp.float32)
            inv_freq = 1.0 / 10000.0 ** (half / DIM_HEAD)
            t = jnp.arange(n, dtype=jnp.float32)
            freqs = t[:, None] * inv_freq[None, :]
            freqs = jnp.concatenate([freqs, freqs], -1)
            base_scale = (half + 0.4 * DIM_HEAD) / (1.4 * DIM_HEAD)
            power = (t - n // 2) / (WINDOW // 2)
            scale = base_scale[None, :] ** power[:, None]
            scale = jnp.concatenate([scale, scale], -1)
            return (freqs, scale)

        def local_attention(q, k, v):
            b, h, n, d = q.shape
            w = WINDOW
            nw = n // w
            bq = q.reshape(b, h, nw, w, d)
            bk = k.reshape(b, h, nw, w, d)
            bv = v.reshape(b, h, nw, w, d)

            def look(t):
                p = jnp.pad(t, ((0, 0), (0, 0), (1, 0), (0, 0), (0, 0)))
                return jnp.concatenate([p[:, :, :nw], p[:, :, 1:]], axis=3)
            bk2, bv2 = (look(bk), look(bv))
            seq = jnp.arange(n).reshape(nw, w)
            seq_p = jnp.pad(seq, ((1, 0), (0, 0)), constant_values=-1)
            jt = jnp.concatenate([seq_p[:nw], seq_p[1:]], axis=1)
            it = seq[:, :, None]
            jb = jt[:, None, :]
            mask = (it < jb) | (it > jb + w) | (jb == -1)
            sim = jnp.einsum('bhwie,bhwje->bhwij', bq, bk2) * QK_SCALE
            sim = jnp.where(mask, -jnp.finfo(sim.dtype).max, sim)
            attn = jax.nn.softmax(sim, -1)
            out = jnp.einsum('bhwij,bhwje->bhwie', attn, bv2)
            return out.reshape(b, h, n, d)

        def attn_layer(x, Wqkv, qs, ksc, Wo):
            b, n, _ = x.shape
            qkv = x @ Wqkv
            q, k, v = jnp.split(qkv, 3, -1)
            sh = lambda t: t.reshape(b, n, HEADS, DIM_HEAD).transpose(0, 2, 1, 3)
            q, k, v = (sh(q), sh(k), sh(v))
            q = l2norm(q) * qs
            k = l2norm(k) * ksc
            freqs, scale = rotary_tables(n)
            cos, sin = (jnp.cos(freqs), jnp.sin(freqs))
            q = q * cos * scale + rotate_half(q) * sin * scale
            inv = 1.0 / scale
            k = k * cos * inv + rotate_half(k) * sin * inv
            out = local_attention(q, k, v)
            out = out.transpose(0, 2, 1, 3).reshape(b, n, INNER)
            return out @ Wo

        def ffn_layer(x, g, bln, W1, b1, W2, b2):
            mu = x.mean(-1, keepdims=True)
            var = ((x - mu) ** 2).mean(-1, keepdims=True)
            xn = (x - mu) / jnp.sqrt(var + 1e-05) * g + bln
            hg = xn @ W1 + b1
            a, gate = jnp.split(hg, 2, -1)
            return a * jax.nn.gelu(gate, approximate=False) @ W2 + b2
        key = jax.random.key(seed)
        ks = jax.random.split(key, 8)
        B, N = (2, 256)
        init = lambda k, shape: jax.random.normal(k, shape, jnp.float32) * 0.02
        return {'x': jax.random.normal(ks[0], (B, N, DIM), jnp.float32), 'Wqkv': init(ks[1], (DEPTH, DIM, 3 * INNER)), 'q_scale': jnp.ones((DEPTH, DIM_HEAD), jnp.float32), 'k_scale': jnp.ones((DEPTH, DIM_HEAD), jnp.float32), 'Wo': init(ks[2], (DEPTH, INNER, DIM)), 'ln_g': jnp.ones((DEPTH, DIM), jnp.float32), 'ln_b': jnp.zeros((DEPTH, DIM), jnp.float32), 'W1': init(ks[3], (DEPTH, DIM, 2 * DIM_INNER)), 'b1': jnp.zeros((DEPTH, 2 * DIM_INNER), jnp.float32), 'W2': init(ks[4], (DEPTH, DIM_INNER, DIM)), 'b2': jnp.zeros((DEPTH, DIM), jnp.float32)}
    _L0_ffn_in = _L0_ffn_setup()
    _d = {'L0_attn_x': _L0_attn_in['x'], 'L0_attn_Wq': _L0_attn_in['Wq'], 'L0_attn_Wk': _L0_attn_in['Wk'], 'L0_attn_Wv': _L0_attn_in['Wv'], 'L0_attn_Wo': _L0_attn_in['Wo'], 'L0_attn_gn_weight': _L0_attn_in['gn_weight'], 'L0_attn_gn_bias': _L0_attn_in['gn_bias'], 'L0_ffn_Wqkv': _L0_ffn_in['Wqkv'], 'L0_ffn_q_scale': _L0_ffn_in['q_scale'], 'L0_ffn_k_scale': _L0_ffn_in['k_scale'], 'L0_ffn_Wo': _L0_ffn_in['Wo'], 'L0_ffn_ln_g': _L0_ffn_in['ln_g'], 'L0_ffn_ln_b': _L0_ffn_in['ln_b'], 'L0_ffn_W1': _L0_ffn_in['W1'], 'L0_ffn_b1': _L0_ffn_in['b1'], 'L0_ffn_W2': _L0_ffn_in['W2'], 'L0_ffn_b2': _L0_ffn_in['b2']}
    _x0 = _d['L0_attn_x']
    _d['L0_attn_x'] = jax.random.normal(jax.random.fold_in(jax.random.key(seed), 1), (1, 2048, 128), dtype=_x0.dtype)
    del _x0
    return _d

def reference(L0_attn_x, L0_attn_Wq, L0_attn_Wk, L0_attn_Wv, L0_attn_Wo, L0_attn_gn_weight, L0_attn_gn_bias, L0_ffn_Wqkv, L0_ffn_q_scale, L0_ffn_k_scale, L0_ffn_Wo, L0_ffn_ln_g, L0_ffn_ln_b, L0_ffn_W1, L0_ffn_b1, L0_ffn_W2, L0_ffn_b2):

    def _L0_attn_ref(x, Wq, Wk, Wv, Wo, gn_weight, gn_bias):
        import math
        import jax, jax.numpy as jnp
        import numpy as np
        N_HEADS = 8
        EPS = 1e-05
        B, L, D = x.shape
        H = N_HEADS
        dh = D // H
        gammas = 1.0 - jnp.exp(jnp.linspace(math.log(1.0 / 32.0), math.log(1.0 / 512.0), H)).astype(x.dtype)

        def proj(W):
            return (x @ W.T).reshape(B, L, H, dh).transpose(1, 0, 2, 3)
        qT, kT, vT = (proj(Wq), proj(Wk), proj(Wv))
        g = gammas[None, :, None, None]

        def step(S, qkv_t):
            q_t, k_t, v_t = qkv_t
            S = g * S + k_t[..., :, None] * v_t[..., None, :]
            y_t = jnp.einsum('bhde,bhd->bhe', S, q_t)
            return (S, y_t)
        S0 = jnp.zeros((B, H, dh, dh), dtype=x.dtype)
        _, ys = jax.lax.scan(step, S0, (qT, kT, vT))
        out = ys.transpose(1, 0, 2, 3)
        mean = out.mean(axis=(1, 3), keepdims=True)
        var = out.var(axis=(1, 3), keepdims=True)
        out = (out - mean) * jax.lax.rsqrt(var + EPS)
        out = out.reshape(B, L, D) * gn_weight + gn_bias
        return out @ Wo.T

    def _L0_ffn_ref(x, Wqkv, q_scale, k_scale, Wo, ln_g, ln_b, W1, b1, W2, b2):
        import jax, jax.numpy as jnp
        import numpy as np
        DIM = 128
        DEPTH = 6
        HEADS = 16
        DIM_HEAD = 64
        WINDOW = 32
        INNER = HEADS * DIM_HEAD
        DIM_INNER = int(DIM * 4 * 2 / 3)
        QK_SCALE = 8.0

        def shift_tokens(t):
            a, s = jnp.split(t, 2, -1)
            s = jnp.pad(s, ((0, 0), (1, 0), (0, 0)))[:, :-1]
            return jnp.concatenate([a, s], -1)

        def l2norm(t):
            return t / jnp.maximum(jnp.linalg.norm(t, axis=-1, keepdims=True), 1e-12)

        def rotate_half(x):
            x1, x2 = jnp.split(x, 2, -1)
            return jnp.concatenate([-x2, x1], -1)

        def rotary_tables(n):
            half = jnp.arange(0, DIM_HEAD, 2, dtype=jnp.float32)
            inv_freq = 1.0 / 10000.0 ** (half / DIM_HEAD)
            t = jnp.arange(n, dtype=jnp.float32)
            freqs = t[:, None] * inv_freq[None, :]
            freqs = jnp.concatenate([freqs, freqs], -1)
            base_scale = (half + 0.4 * DIM_HEAD) / (1.4 * DIM_HEAD)
            power = (t - n // 2) / (WINDOW // 2)
            scale = base_scale[None, :] ** power[:, None]
            scale = jnp.concatenate([scale, scale], -1)
            return (freqs, scale)

        def local_attention(q, k, v):
            b, h, n, d = q.shape
            w = WINDOW
            nw = n // w
            bq = q.reshape(b, h, nw, w, d)
            bk = k.reshape(b, h, nw, w, d)
            bv = v.reshape(b, h, nw, w, d)

            def look(t):
                p = jnp.pad(t, ((0, 0), (0, 0), (1, 0), (0, 0), (0, 0)))
                return jnp.concatenate([p[:, :, :nw], p[:, :, 1:]], axis=3)
            bk2, bv2 = (look(bk), look(bv))
            seq = jnp.arange(n).reshape(nw, w)
            seq_p = jnp.pad(seq, ((1, 0), (0, 0)), constant_values=-1)
            jt = jnp.concatenate([seq_p[:nw], seq_p[1:]], axis=1)
            it = seq[:, :, None]
            jb = jt[:, None, :]
            mask = (it < jb) | (it > jb + w) | (jb == -1)
            sim = jnp.einsum('bhwie,bhwje->bhwij', bq, bk2) * QK_SCALE
            sim = jnp.where(mask, -jnp.finfo(sim.dtype).max, sim)
            attn = jax.nn.softmax(sim, -1)
            out = jnp.einsum('bhwij,bhwje->bhwie', attn, bv2)
            return out.reshape(b, h, n, d)

        def attn_layer(x, Wqkv, qs, ksc, Wo):
            b, n, _ = x.shape
            qkv = x @ Wqkv
            q, k, v = jnp.split(qkv, 3, -1)
            sh = lambda t: t.reshape(b, n, HEADS, DIM_HEAD).transpose(0, 2, 1, 3)
            q, k, v = (sh(q), sh(k), sh(v))
            q = l2norm(q) * qs
            k = l2norm(k) * ksc
            freqs, scale = rotary_tables(n)
            cos, sin = (jnp.cos(freqs), jnp.sin(freqs))
            q = q * cos * scale + rotate_half(q) * sin * scale
            inv = 1.0 / scale
            k = k * cos * inv + rotate_half(k) * sin * inv
            out = local_attention(q, k, v)
            out = out.transpose(0, 2, 1, 3).reshape(b, n, INNER)
            return out @ Wo

        def ffn_layer(x, g, bln, W1, b1, W2, b2):
            mu = x.mean(-1, keepdims=True)
            var = ((x - mu) ** 2).mean(-1, keepdims=True)
            xn = (x - mu) / jnp.sqrt(var + 1e-05) * g + bln
            hg = xn @ W1 + b1
            a, gate = jnp.split(hg, 2, -1)
            return a * jax.nn.gelu(gate, approximate=False) @ W2 + b2
        for i in range(DEPTH):
            x = attn_layer(shift_tokens(x), Wqkv[i], q_scale[i], k_scale[i], Wo[i]) + x
            x = ffn_layer(shift_tokens(x), ln_g[i], ln_b[i], W1[i], b1[i], W2[i], b2[i]) + x
        return x
    x = L0_attn_x
    x = x + 0.5 * _L0_ffn_ref(_layernorm(x, axis=-1), L0_ffn_Wqkv, L0_ffn_q_scale, L0_ffn_k_scale, L0_ffn_Wo, L0_ffn_ln_g, L0_ffn_ln_b, L0_ffn_W1, L0_ffn_b1, L0_ffn_W2, L0_ffn_b2)
    x = x + _L0_attn_ref(_layernorm(x, axis=-1), L0_attn_Wq, L0_attn_Wk, L0_attn_Wv, L0_attn_Wo, L0_attn_gn_weight, L0_attn_gn_bias)
    x = x + 0.5 * _L0_ffn_ref(_layernorm(x, axis=-1), L0_ffn_Wqkv, L0_ffn_q_scale, L0_ffn_k_scale, L0_ffn_Wo, L0_ffn_ln_g, L0_ffn_ln_b, L0_ffn_W1, L0_ffn_b1, L0_ffn_W2, L0_ffn_b2)
    return x

_drawn_inputs = setup_inputs


def setup_inputs(seed=0):
    import zlib

    import numpy as np

    out = dict(_drawn_inputs(seed))
    spreads = {'L0_attn_gn_weight': (1.0, 0.541),
     'L0_attn_gn_bias': (0.0, 0.586),
     'L0_ffn_q_scale': (1.0, 0.6),
     'L0_ffn_k_scale': (1.0, 0.6),
     'L0_ffn_ln_g': (1.0, 0.6),
     'L0_ffn_ln_b': (0.0, 0.8),
     'L0_ffn_b1': (0.0, 0.8),
     'L0_ffn_b2': (0.0, 0.1)}
    factors = {'L0_ffn_W1': 3.162, 'L0_ffn_W2': 3.101}
    for name, (base, spread) in spreads.items():
        noise = np.random.default_rng([zlib.crc32(name.encode()), seed]).standard_normal(out[name].shape)
        drawn = base * np.exp(spread * noise) if base else spread * noise
        out[name] = jnp.asarray(drawn.astype(out[name].dtype))
    for name, factor in factors.items():
        out[name] = (out[name] * factor).astype(out[name].dtype)
    return out
```

```python
import concourse.bass as bass
from concourse import mybir
from contextlib import ExitStack

P = 128
NTOK = 2048
DEPTH = 6
HEADS, DHEAD = 16, 64
INNER = HEADS * DHEAD
WIN = 32
CH = INNER // P
GT = 512
NG = NTOK // GT
TPG = GT // P
NT = NTOK // P
UPT = 4
UPG = UPT * TPG
HID = 341
HCH = [(0, 128), (128, 128), (256, HID - 256)]
VW = DHEAD + 1
KCOLS = P + WIN
RH = 8
RD = P // RH


def build_macaron(nc, x, w_attn, w_out, prm_attn, w1, w2, prm_ffn, w_ret, gn, tables, norm_in,
                  norm_out, consts, mask_n, mask_t, sel, dec_a, dec_v, out):
    fp32, bf16, f32r = mybir.dt.float32, mybir.dt.bfloat16, mybir.dt.float32r
    ACT, ALU, AX = mybir.ActivationFunctionType, mybir.AluOpType, mybir.AxisListType
    LN_SCALE = 2.0 ** 16
    ctx = ExitStack()
    with ctx:
        def sb(name, shape, dt=fp32):
            return ctx.enter_context(nc.sbuf_tensor(name, shape, dt))

        def sem(name):
            return ctx.enter_context(nc.semaphore(name))

        PA = ctx.enter_context(nc.psum_tensor("PA", [P, 4, 512], fp32))
        PB = ctx.enter_context(nc.psum_tensor("PB", [P, 4, 512], fp32))
        SN = PB[:, 2:4, :]

        X = sb("X", [P, NTOK])
        Y = sb("Y", [P, 1 + NTOK])
        Y2 = sb("Y2", [P, 1 + NTOK])
        TAB = sb("TAB", [P, 4, NTOK])
        WA = sb("WA", [P, 5 * INNER])
        WO = sb("WO", [P, CH, P])
        PRA = sb("PRA", [P, 4])
        W1 = sb("W1", [P, 2 * HID])
        W2 = sb("W2", [P, 3, P])
        PRF = sb("PRF", [P, 9])
        XG = sb("XG", [P, GT])
        T1 = sb("T1", [P, 2, GT])
        T2 = sb("T2", [P, 2, GT])
        SQ = sb("SQ", [P, 8, GT])
        QT = sb("QT", [P, CH, GT])
        KT = sb("KT", [P, CH, WIN + GT])
        NR, LT, RN = SQ[:, 0, :], SQ[:, 1, :], SQ[:, 2, :]
        RHI = sb("RHI", [P, GT], f32r)
        RLO = sb("RLO", [P, GT], f32r)
        NI = sb("NI", [P, 4, 32])
        NO = sb("NO", [P, 2 * CH, P], f32r)
        VT = sb("VT", [P, 1 + TPG, HEADS, VW])
        PT = sb("PT", [P, 2, 4, KCOLS])
        RC = sb("RC", [P, 2, 4])
        ON = sb("ON", [P, 2, 4, DHEAD])
        OT = sb("OT", [P, CH, GT])
        NM = sb("NM", [P, HEADS], bf16)
        MT = sb("MT", [P, KCOLS], bf16)
        SEL = sb("SEL", [P, HEADS, P], bf16)
        MASKN = sb("MASKN", [P, 1 + NG, 2 * WIN], bf16)
        MASKT = sb("MASKT", [P, 1 + NG, KCOLS], bf16)
        IDB = sb("IDB", [P, P], bf16)
        CST = sb("CST", [P, 2, P])
        EPS = sb("EPS", [P, 1])
        LNB = sb("LNB", [P, 1])
        RST = sb("RST", [P, 24])
        GN = sb("GN", [P, 3])
        XF = OT[:, 0:4, :]
        XC = OT[:, 4:8, :]
        GE = T1
        HB = SQ[:, 4:8, :]
        XNAT = QT[:, 0:4, :].rearrange("p a (b c) -> p (a b) c", c=P)

        s_c_in = sem("s_c_in")
        s_x_in = sem("s_x_in")
        s_wa_in = sem("s_wa_in")
        s_wo_in = sem("s_wo_in")
        s_wf_in = sem("s_wf_in")
        s_ret_in = sem("s_ret_in")
        s_xt_ps = sem("s_xt_ps")
        s_xt = sem("s_xt")
        s_no = sem("s_no")
        s_cst = sem("s_cst")
        s_xg = sem("s_xg")
        s_vc = sem("s_vc")
        s_kc = sem("s_kc")
        s_pair = sem("s_pair")
        s_t1 = sem("s_t1")
        s_t2 = sem("s_t2")
        s_add = sem("s_add")
        s_sq = sem("s_sq")
        s_nb = sem("s_nb")
        s_nr = sem("s_nr")
        s_ln = sem("s_ln")
        s_rn = sem("s_rn")
        s_hi = sem("s_hi")
        s_lo = sem("s_lo")
        s_v = sem("s_v")
        s_vev = sem("s_vev")
        s_rb = sem("s_rb")
        s_qk = sem("s_qk")
        s_sn = sem("s_sn")
        s_mx = sem("s_mx")
        s_mtp = sem("s_mtp")
        s_mt = sem("s_mt")
        s_st = sem("s_st")
        s_ex = sem("s_ex")
        s_pv = sem("s_pv")
        s_rc = sem("s_rc")
        s_on = sem("s_on")
        s_tr = sem("s_tr")
        s_ot = sem("s_ot")
        s_wo = sem("s_wo")
        s_y2 = sem("s_y2")
        s_mu = sem("s_mu")
        s_xc = sem("s_xc")
        s_lsq = sem("s_lsq")
        s_var = sem("s_var")
        s_lln = sem("s_lln")
        s_lrs = sem("s_lrs")
        s_ldm = sem("s_ldm")
        s_lna = sem("s_lna")
        s_xf = sem("s_xf")
        s_f1 = sem("s_f1")
        s_ge = sem("s_ge")
        s_h = sem("s_h")
        s_f2 = sem("s_f2")
        s_yf = sem("s_yf")
        s_xs = sem("s_xs")
        s_rwt = sem("s_rwt")
        s_rwe = sem("s_rwe")
        s_zg = sem("s_zg")
        s_rq = sem("s_rq")
        s_rqe = sem("s_rqe")
        s_rkv = sem("s_rkv")
        s_rkve = sem("s_rkve")
        s_rqd = sem("s_rqd")
        s_rkd = sem("s_rkd")
        s_qm = sem("s_qm")
        s_ra = sem("s_ra")
        s_am = sem("s_am")
        s_ry = sem("s_ry")
        s_ru = sem("s_ru")
        s_rss = sem("s_rss")
        s_rsb = sem("s_rsb")
        s_yn = sem("s_yn")
        s_yt = sem("s_yt")
        s_rtr = sem("s_rtr")
        s_gs1 = sem("s_gs1")
        s_gs1p = sem("s_gs1p")
        s_gs2 = sem("s_gs2")
        s_gs2p = sem("s_gs2p")
        s_gs4 = sem("s_gs4")
        s_gs5 = sem("s_gs5")
        s_gs6 = sem("s_gs6")
        s_gy = sem("s_gy")
        s_ro = sem("s_ro")
        s_rox = sem("s_rox")
        s_fin_ps = sem("s_fin_ps")
        s_fin = sem("s_fin")
        s_out_done = sem("s_out_done")
        s_dchain = sem("s_dchain")
        s_achain = sem("s_achain")
        block = ctx.enter_context(nc.Block())

        primed = (s_v, s_y2, s_yf, s_pv, s_wo, s_nb, s_t2, s_sq, s_add, s_ex, s_tr, s_h, s_f2, s_mtp, s_mx, s_ra, s_rkv, s_rkve, s_yt, s_am, s_rsb, s_yn)

        IDF, AVG = CST[:, 0, :], CST[:, 1, :]

        RW = QT[:, 0, :].rearrange("p (a n) -> p a n", a=4)
        DA = QT[:, 1:3, :].rearrange("p a (b n) -> p (a b) n", n=P)
        DV = QT[:, 3:6, :].rearrange("p a n -> p (a n)")[:, 0:10 * P].rearrange("p (a n) -> p a n", n=P)
        DQ, DK, HM = DV[:, 0, :], DV[:, 1, :], DV[:, 2:10, :]
        BLK = QT[:, 7, 0:2 * P].rearrange("p (a n) -> p a n", a=2)
        B16, BDG = BLK[:, 0, :], BLK[:, 1, :]
        RWT = QT[:, 6, :].rearrange("p (a n) -> p a n", a=4)
        KR, QR, QD = KT[:, 0, 0:GT], KT[:, 1, 0:GT], KT[:, 2, 0:GT]
        KV = KT[:, 3:6, :].rearrange("p a n -> p (a n)")[:, 0:1024].rearrange("p (a n) -> p a n", a=4)
        KD = KT[:, 6, 0:GT].rearrange("p (a n) -> p a n", a=4)
        ZG = XG[:, :]
        QM = SQ[:, 0:2, :].rearrange("p a (b n) -> p (a b) n", n=P)
        AM = SQ[:, 2:4, :]
        SS, SB, YN = SQ[:, 4, 0:P], SQ[:, 4, P:2 * P], SQ[:, 4, 2 * P:3 * P]

        stack_now = [0]

        def ln_number(L):
            return L + 1 if stack_now[0] == 0 else L + 3

        order = ["v"] * 8 + [("m", 0)]
        for t in range(TPG):
            order += [("pv", 4 * t), ] + ([("tr", 4 * t - 1)] if t else [])
            order += [("pv", 4 * t + 1), ("tr", 4 * t), ("pv", 4 * t + 2), ("tr", 4 * t + 1), ("pv", 4 * t + 3)]
            if t + 1 < TPG:
                order += [("m", t + 1)]
            order += [("tr", 4 * t + 2)]
        order += [("tr", 4 * TPG - 1)]
        assert len(order) % 2 == 0

        def bank(use):
            return PB[:, order.index(use) % 2, :]

        def tr_bank(n):
            return bank(("tr", n))

        @block.sync
        def _(sp):
            sp.dma_start(XNAT, x[0].rearrange("(t p) c -> p t c", p=P)).then_inc(s_x_in, 16)
            sp.dma_start(CST[:, :, :], consts[:, 0:2, :]).then_inc(s_c_in, 16)
            sp.dma_start(NI[:, :, :], norm_in).then_inc(s_c_in, 16)
            sp.dma_start(SQ[:, 0:4, :].rearrange("p a n -> p (a n)"),
                         norm_out.rearrange("p a n -> p (a n)")).then_inc(s_c_in, 16)
            sp.dma_start(GN[:, :], gn).then_inc(s_c_in, 16)
            sp.dma_start(MASKN[:, :, :], mask_n).then_inc(s_c_in, 16)
            sp.dma_start(MASKT[:, :, :], mask_t).then_inc(s_c_in, 16)
            sp.dma_start(SEL[:, :, :], sel[:, 0:HEADS, :]).then_inc(s_c_in, 16)
            sp.dma_start(IDB[:, :], sel[:, HEADS, :]).then_inc(s_c_in, 16)

            def stack_weights(s):
                with sp.Fori(0, DEPTH) as l:
                    L = l + s * DEPTH
                    sp.wait_ge(s_v, 1 + L * (8 * NG))
                    sp.dma_start(WA[:, :], w_attn[bass.ds(l, 1)].rearrange("a p n -> (a p) n")).then_inc(s_wa_in, 16)
                    sp.dma_start(PRA[:, :], prm_attn[bass.ds(l, 1)].rearrange("a p n -> (a p) n")).then_inc(s_wa_in, 16)
                    sp.wait_ge(s_y2, 1 + L * NG)
                    sp.dma_start(WO[:, :, :].rearrange("p a n -> p (a n)"),
                                 w_out[bass.ds(l, 1)].rearrange("a p n -> (a p) n")).then_inc(s_wo_in, 16)
                    sp.wait_ge(s_yf, 1 + L * NG)
                    sp.dma_start(W1[:, :], w1[bass.ds(l, 1)].rearrange("a p n -> (a p) n")).then_inc(s_wf_in, 16)
                    sp.dma_start(W2[:, :, :].rearrange("p a n -> p (a n)"),
                                 w2[bass.ds(l, 1)].rearrange("a p n -> (a p) n")).then_inc(s_wf_in, 16)
                    sp.dma_start(PRF[:, :], prm_ffn[bass.ds(l, 1)].rearrange("a p n -> (a p) n")).then_inc(s_wf_in, 16)

            sp.dma_start(TAB[:, :, :], tables).then_inc(s_c_in, 16)
            stack_weights(0)
            sp.wait_ge(s_y2, 1 + DEPTH * NG)
            sp.wait_ge(s_yf, 1 + DEPTH * NG)
            sp.dma_start(RW[:, :, :], w_ret).then_inc(s_ret_in, 16)
            sp.dma_start(BLK, consts[:, 2:4, :]).then_inc(s_ret_in, 16)
            sp.dma_start(DA[:, :, :], dec_a).then_inc(s_ret_in, 16)
            sp.dma_start(DV[:, :, :], dec_v).then_inc(s_ret_in, 16)
            stack_weights(1)
            sp.wait_ge(s_fin, 4)
            sp.dma_start(out[0].rearrange("(t p) c -> p t c", p=P), XNAT).then_inc(s_out_done, 16)
            sp.wait_ge(s_out_done, 16)

        def ln_pe(pe, n, src):
            for g in range(NG):
                nc.tensor.matmul(PA[:, g, :], AVG, src(g), start=True, stop=True).then_inc(s_mu, 1)
            for g in range(NG):
                pe.wait_ge(s_lsq, n * NG + g + 1)
                nc.tensor.matmul(PB[:, g, :], AVG, SQ[:, g, :], start=True, stop=True).then_inc(s_var, 1)

        def ln_dve(ve, n, src, dst, affine):
            for g in range(NG):
                ve.wait_ge(s_mu, n * NG + g + 1)
                nc.vector.tensor_tensor(XC[:, g, :], src(g), PA[:, g, :], ALU.subtract).then_inc(s_xc, 1)
            for g in range(NG):
                ve.wait_ge(s_lrs, n * NG + g + 1)
                nc.vector.tensor_tensor(dst(g), XC[:, g, :], SQ[:, g, :], ALU.mult).then_inc(s_ldm, 1)
            if affine is not None:
                for g in range(NG):
                    ve.wait_ge(s_ldm, n * NG + g + 1)
                    nc.vector.tensor_scalar(dst(g), dst(g), PRF[:, 0:1], PRF[:, 1:2], ALU.mult, ALU.add)\
                        .then_inc(s_lna, 1)

        def ln_act(ac, n):
            for g in range(NG):
                ac.wait_ge(s_xc, n * NG + g + 1)
                nc.scalar.activation(SQ[:, g, :], XC[:, g, :], ACT.Square).then_inc(s_lsq, 1)
            for g in range(NG):
                ac.wait_ge(s_var, n * NG + g + 1)
                nc.scalar.activation(SQ[:, g, :], PB[:, g, :], ACT.Ln, bias=EPS[:, 0:1]).then_inc(s_lln, 1)
                ac.wait_ge(s_lln, n * NG + g + 1)
                nc.scalar.activation(SQ[:, g, :], SQ[:, g, :], ACT.Exp, scale=-0.5).then_inc(s_lrs, 1)

        def x_group(g):
            return X[:, g * GT:(g + 1) * GT]

        def y_group(g):
            return Y[:, 1 + g * GT:1 + (g + 1) * GT]

        def xf_group(g):
            return XF[:, g, :]

        def xc_group(g):
            return XC[:, g, :]

        @block.gpsimd
        def _(po):
            for started in primed:
                po.sem_inc(started, 1)
            po.memset(Y[:, 0:1], 0.0).then_inc(s_cst, 1)
            po.memset(Y2[:, 0:1], 0.0).then_inc(s_cst, 1)
            po.memset(KT[:, :, :], 0.0).then_inc(s_cst, 1)
            po.memset(VT[:, :, :, 0:DHEAD], 0.0).then_inc(s_cst, 1)
            po.memset(VT[:, :, :, DHEAD:VW], 1.0).then_inc(s_cst, 1)
            po.memset(MT[:, :], 0.0).then_inc(s_cst, 1)
            po.memset(EPS[:, :], 1e-5).then_inc(s_cst, 1)
            po.memset(LNB[:, :], 8.0 * 0.6931471805599453).then_inc(s_cst, 1)

            def attn_group(i):
                for p in range(2 * CH):
                    if p == CH:
                        po.wait_ge(s_kc, i + 1)
                    po.wait_ge(s_t2, 1 + i * 16 + p + 1)
                    dst = QT[:, p, :] if p < CH else KT[:, p - CH, WIN:WIN + GT]
                    po.tensor_tensor(dst, T1[:, p % 2, :], T2[:, p % 2, :], ALU.add).then_inc(s_add, 1)

            for s in range(2):
                with po.Fori(0, DEPTH) as l:
                    with po.Fori(0, NG) as g:
                        attn_group((l + s * DEPTH) * NG + g)

        @block.scalar
        def _(ac):
            def attn_group(i, g, L):
                ac.wait_ge(s_yf, 1 + L * NG)
                ac.wait_ge(s_v, 1 + i * 8)
                for lo, back in ((0, 0), (64, 1)):
                    nc.scalar.activation(XG[lo:lo + 64, :], Y[lo:lo + 64, bass.ds(g * GT + 1 - back, GT)],
                                         ACT.Copy).then_inc(s_xg, 1)
                ac.wait_ge(s_pv, 1 + i * UPG)
                nc.scalar.activation(VT[:, 0, :, 0:DHEAD], VT[:, TPG, :, 0:DHEAD], ACT.Copy).then_inc(s_vc, 1)
                nc.scalar.activation(KT[:, :, 0:WIN], KT[:, :, GT:GT + WIN], ACT.Copy).then_inc(s_kc, 1)
                for p in range(2 * CH):
                    ac.wait_ge(s_t1, i * 16 + p + 1)
                    ac.wait_ge(s_nb, 1 + i * 4 + ((p - 8) // 4 + 1 if p >= 8 else 0))
                    nc.scalar.activation(SQ[:, p % 8, :], PA[:, 2 * (p % 2), :], ACT.Square).then_inc(s_sq, 1)
                ac.wait_ge(s_nr, i + 1)
                nc.scalar.activation(LT, NR, ACT.Ln, scale=LN_SCALE).then_inc(s_ln, 1)
                ac.wait_ge(s_ln, i + 1)
                nc.scalar.activation(RN, LT, ACT.Exp, scale=-0.5, bias=LNB[:, 0:1]).then_inc(s_rn, 1)
                ac.wait_ge(s_vc, i + 1)
                for n in range(2 * TPG):
                    t, half = n // 2, n % 2
                    ac.wait_ge(s_v, 1 + i * 8 + n + 1)
                    nc.scalar.activation(VT[:, t + 1, 8 * half:8 * half + 8, 0:DHEAD],
                                         PB[:, n % 2, :].rearrange("p (h d) -> p h d", d=DHEAD),
                                         ACT.Copy).then_inc(s_vev, 1)

                def exps(n):
                    ac.wait_ge(s_st, i * UPG + n + 1)
                    ac.wait_ge(s_pv, 1 + i * UPG + n - 1 if n >= 2 else i * UPG)
                    b = n % 2
                    nc.scalar.activation(PT[:, b, :, :].rearrange("p (e c) n -> p e (c n)", e=2),
                                         PA[:, 2 * b:2 * b + 2, 0:2 * KCOLS], ACT.Exp, scale=8.0).then_inc(s_ex, 1)

                def out_copy(n):
                    t, u = n // UPT, n % UPT
                    ac.wait_ge(s_tr, 1 + i * UPG + n + 1)
                    nc.scalar.activation(OT[:, 2 * u:2 * u + 2, t * P:(t + 1) * P],
                                         tr_bank(n)[:, 0:2 * P].rearrange("p (c n) -> p c n", c=2),
                                         ACT.Copy).then_inc(s_ot, 1)

                ac.wait_ge(s_wo, 1 + i)
                for t in range(TPG):
                    n = t * UPT
                    exps(n)
                    if t:
                        out_copy(n - 1)
                    exps(n + 1)
                    exps(n + 2)
                    out_copy(n)
                    exps(n + 3)
                    out_copy(n + 1)
                    out_copy(n + 2)
                out_copy(UPG - 1)

            def ffn(L):
                ln_act(ac, ln_number(L))
                for k in range(3 * NG):
                    g, m = k // 3, k % 3
                    w = HCH[m][1]
                    ac.wait_ge(s_f1, L * 12 + k + 1)
                    ac.wait_ge(s_h, 1 + L * 12 + k - 1 if k >= 2 else L * 12)
                    nc.scalar.activation(GE[0:w, k % 2, :], PA[0:w, 2 * (k % 2), :], ACT.Gelu,
                                         bias=PRF[0:w, 5 + m:6 + m]).then_inc(s_ge, 1)

            def stack(s):
                stack_now[0] = s
                ln_act(ac, 0 if s == 0 else 8)
                ac.wait_ge(s_ldm, NG * (1 if s == 0 else 9))
                with ac.Fori(0, DEPTH) as l:
                    L = l + s * DEPTH
                    with ac.Fori(0, NG) as g:
                        attn_group(L * NG + g, g, L)
                    ffn(L)

            ac.wait_ge(s_cst, 8)
            stack(0)
            ln_act(ac, 7)
            ac.wait_ge(s_rwt, 1)
            nc.scalar.activation(RWT, PA[:, 0, :].rearrange("p (a n) -> p a n", a=4), ACT.Copy).then_inc(s_rwe, 1)
            ac.wait_ge(s_ldm, NG * 8)
            with ac.Fori(0, NG) as r:
                ac.wait_ge(s_rkv, 1 + r)
                nc.scalar.activation(ZG, Y[:, bass.ds(r * GT + 1, GT)], ACT.Copy).then_inc(s_zg, 1)
                ac.wait_ge(s_rq, r + 1)
                ac.wait_ge(s_ra, 1 + r * 4)
                nc.scalar.activation(KR, PA[:, 1, :], ACT.Copy).then_inc(s_rqe, 1)
                nc.scalar.activation(QR, PA[:, 0, :], ACT.Copy).then_inc(s_rqe, 1)
                ac.wait_ge(s_rkv, 1 + r + 1)
                nc.scalar.activation(KV.rearrange("p (b a) n -> p b (a n)", b=2), PA[:, 2:4, :],
                                     ACT.Copy).then_inc(s_rkve, 1)
                for c in range(4):
                    ac.wait_ge(s_ry, r * 4 + c + 1)
                    nc.scalar.activation(YN, PB[:, 2, 0:P], ACT.Copy).then_inc(s_yn, 1)
                    ac.wait_ge(s_rtr, r * 4 + c + 1)
                    nc.scalar.activation(Y2[:, bass.ds(r * GT + 1 + c * P, P)], PA[:, 0, 0:P],
                                         ACT.Copy).then_inc(s_yt, 1)
            ac.wait_ge(s_gs4, 1)
            nc.scalar.activation(RST[:, 10:11], RST[:, 9:10], ACT.Ln, bias=EPS[:, 0:1]).then_inc(s_achain, 1)
            ac.wait_ge(s_achain, 1)
            nc.scalar.activation(RST[:, 11:12], RST[:, 10:11], ACT.Exp, scale=-0.5).then_inc(s_gs5, 1)
            ac.wait_ge(s_gs6, 1)
            for g in range(NG):
                nc.scalar.activation(Y2[:, 1 + g * GT:1 + (g + 1) * GT], Y2[:, 1 + g * GT:1 + (g + 1) * GT],
                                     ACT.Identity, scale=RST[:, 12:13], bias=RST[:, 14:15]).then_inc(s_gy, 1)
            stack(1)

        @block.vector
        def _(ve):
            def attn_group(i, g, L):
                ve.wait_ge(s_wa_in, (L + 1) * 32)
                for p in range(2 * CH):
                    kind, b = p // CH, 2 * (p % 2)
                    ve.wait_ge(s_pair, i * 16 + p + 1)
                    ve.wait_ge(s_add, 1 + i * 16 + (p - 1 if p >= 2 else 0))
                    nc.vector.scalar_tensor_tensor(
                        out=T1[:, p % 2, :], in0=PA[:, b, :], scalar=PRA[:, 2 * kind:2 * kind + 1],
                        in1=TAB[:, 2 * kind, bass.ds(g * GT, GT)], op0=ALU.mult, op1=ALU.mult).then_inc(s_t1, 1)
                    nc.vector.scalar_tensor_tensor(
                        out=T2[:, p % 2, :], in0=PA[:, b + 1, :], scalar=PRA[:, 2 * kind + 1:2 * kind + 2],
                        in1=TAB[:, 2 * kind + 1, bass.ds(g * GT, GT)], op0=ALU.mult, op1=ALU.mult).then_inc(s_t2, 1)
                ve.wait_ge(s_nb, 1 + i * 4 + 4)
                nc.vector.tensor_scalar_max(NR, SN[:, 0, :], 1e-24).then_inc(s_nr, 1)
                ve.wait_ge(s_rn, i + 1)
                nc.vector.tensor_copy(RHI[:, :], RN).then_inc(s_hi, 1)
                ve.wait_ge(s_hi, i + 1)
                nc.vector.tensor_tensor(RLO[:, :], RN, RHI[:, :].bitcast(fp32), ALU.subtract).then_inc(s_lo, 1)
                for p in range(2 * CH):
                    ve.wait_ge(s_rb, i * 16 + p + 1)
                    ve.wait_ge(s_add, 1 + i * 16 + p + 1)
                    dst = QT[:, p, :] if p < CH else KT[:, p - CH, WIN:WIN + GT]
                    nc.vector.tensor_tensor(dst, dst, PA[:, p % 4, :], ALU.mult).then_inc(s_qk, 1)

                def maxima(t):
                    ve.wait_ge(s_sn, i * TPG + t + 1)
                    ve.wait_ge(s_mtp, 1 + i * TPG + t)
                    nc.vector.tensor_reduce(NM[:, :], SN.rearrange("p e (c k) -> p (e c) k", k=2 * WIN),
                                            AX.X, ALU.max, negate=True).then_inc(s_mx, 1)

                def maxima_copy(t):
                    ve.wait_ge(s_mtp, 1 + i * TPG + t + 1)
                    ps = bank(("m", t)).bitcast(bf16)
                    nc.vector.tensor_copy(MT[0:HEADS, 0:P], ps[0:HEADS, 0:P]).then_inc(s_mt, 1)
                    nc.vector.tensor_copy(MT[0:HEADS, P:KCOLS], ps[0:HEADS, 0:WIN]).then_inc(s_mt, 1)

                def normalise(n):
                    ve.wait_ge(s_pv, 1 + i * UPG + n + 1)
                    ve.wait_ge(s_tr, 1 + i * UPG + (n - 1 if n >= 2 else 0))
                    ps = bank(("pv", n))[:, 0:4 * VW].rearrange("p (h d) -> p h d", d=VW)
                    nc.vector.reciprocal(RC[:, n % 2, :].unsqueeze(2), ps[:, :, DHEAD:VW]).then_inc(s_rc, 1)
                    ve.wait_ge(s_rc, i * UPG + n + 1)
                    nc.vector.tensor_tensor(ON[:, n % 2, :, :], ps[:, :, 0:DHEAD],
                                            RC[:, n % 2, :].unsqueeze(2).to_broadcast([P, 4, DHEAD]),
                                            ALU.mult).then_inc(s_on, 1)

                maxima(0)
                maxima_copy(0)
                for t in range(TPG):
                    if t + 1 < TPG:
                        maxima(t + 1)
                    for u in range(UPT):
                        normalise(UPT * t + u)
                    if t + 1 < TPG:
                        maxima_copy(t + 1)
                ve.wait_ge(s_wo, 1 + i + 1)
                nc.vector.tensor_tensor(Y2[:, bass.ds(g * GT + 1, GT)], SN[:, 1, :],
                                        Y[:, bass.ds(g * GT + 1, GT)], ALU.add).then_inc(s_y2, 1)

            def ffn(L):
                ve.wait_ge(s_y2, 1 + (L + 1) * NG)
                nc.vector.memset(KT[:, :, GT:GT + WIN], 0.0)
                for g in range(NG):
                    for lo, back in ((0, 0), (64, 1)):
                        a = g * GT + 1 - back
                        nc.vector.tensor_copy(XF[lo:lo + 64, g, :], Y2[lo:lo + 64, a:a + GT]).then_inc(s_xf, 1)
                ve.wait_ge(s_xf, (L + 1) * 2 * NG)
                ve.wait_ge(s_wf_in, (L + 1) * 48)
                ln_dve(ve, ln_number(L), xf_group, xc_group, True)

                def residual(g):
                    ve.wait_ge(s_f2, 1 + L * 12 + 3 * g + 3)
                    nc.vector.scalar_tensor_tensor(out=y_group(g), in0=PB[:, g % 2, :], scalar=PRF[:, 8:9],
                                                   in1=Y2[:, 1 + g * GT:1 + (g + 1) * GT],
                                                   op0=ALU.add, op1=ALU.add).then_inc(s_yf, 1)

                for k in range(3 * NG):
                    m = k % 3
                    w = HCH[m][1]
                    ve.wait_ge(s_ge, L * 12 + k + 1)
                    ve.wait_ge(s_f2, 1 + L * 12 + (k - 3 if k >= 4 else 0))
                    nc.vector.scalar_tensor_tensor(out=HB[0:w, k % 4, :], in0=PA[0:w, 2 * (k % 2) + 1, :],
                                                   scalar=PRF[0:w, 2 + m:3 + m], in1=GE[0:w, k % 2, :],
                                                   op0=ALU.add, op1=ALU.mult).then_inc(s_h, 1)
                    if k >= 5 and (k - 5) % 3 == 0:
                        residual((k - 5) // 3)
                residual(NG - 1)

            def stack(s):
                stack_now[0] = s
                ln_dve(ve, 0 if s == 0 else 8, x_group, y_group, None)
                with ve.Fori(0, DEPTH) as l:
                    L = l + s * DEPTH
                    with ve.Fori(0, NG) as g:
                        attn_group(L * NG + g, g, L)
                    ffn(L)
                for g in range(NG):
                    ve.wait_ge(s_yf, 1 + (s + 1) * DEPTH * NG)
                    nc.vector.scalar_tensor_tensor(out=x_group(g), in0=y_group(g), scalar=0.5, in1=x_group(g),
                                                   op0=ALU.mult, op1=ALU.add).then_inc(s_xs, 1)

            ve.wait_ge(s_c_in, 16 * 9)
            nc.vector.tensor_copy(NO[:, :, :], SQ[:, 0:4, :].rearrange("p a (b n) -> p (a b) n", n=P)).then_inc(s_no, 1)
            ve.wait_ge(s_xt_ps, 1)
            nc.vector.tensor_copy(X[:, :], PA[:, :, :].rearrange("p a n -> p (a n)")).then_inc(s_xt, 1)
            ve.wait_ge(s_xt, 1)
            ve.wait_ge(s_cst, 8)
            stack(0)
            ve.wait_ge(s_xs, NG)
            ln_dve(ve, 7, x_group, y_group, None)
            nc.vector.memset(SQ[:, 4, 0:2 * P], 0.0).then_inc(s_rss, 1)
            ve.wait_ge(s_ret_in, 64)
            with ve.Fori(0, NG) as r:
                ve.wait_ge(s_rqe, 2 * (r + 1))
                nc.vector.tensor_tensor(QD.rearrange("p (a n) -> p a n", a=4), QR.rearrange("p (a n) -> p a n", a=4),
                                        DQ.unsqueeze(1).to_broadcast([P, 4, P]), ALU.mult).then_inc(s_rqd, 1)
                ve.wait_ge(s_rkve, 1 + r + 1)
                nc.vector.tensor_tensor(KD, KV[:, :, 0:P], DK.unsqueeze(1).to_broadcast([P, 4, P]),
                                        ALU.mult).then_inc(s_rkd, 1)
                for c in range(4):
                    n = r * 4 + c
                    ve.wait_ge(s_ra, 1 + n)
                    nc.vector.tensor_tensor(QM, QR[:, c * P:(c + 1) * P].unsqueeze(1).to_broadcast([P, RH, P]), HM,
                                            ALU.mult).then_inc(s_qm, 1)
                    ve.wait_ge(s_ra, 1 + n + 1)
                    nc.vector.tensor_tensor(AM, PB[:, 0:2, :], DA.rearrange("p (b a) n -> p b (a n)", b=2),
                                            ALU.mult).then_inc(s_am, 1)
                    ve.wait_ge(s_ru, n + 1)
                    ve.wait_ge(s_rss, n + 1)
                    nc.vector.scalar_tensor_tensor(out=SS, in0=SS, scalar=GN[:, 2:3], in1=PB[:, 3, 0:P],
                                                   op0=ALU.mult, op1=ALU.add).then_inc(s_rss, 1)
                    ve.wait_ge(s_rss, n + 2)
                    nc.vector.tensor_tensor(SB, SS, BDG, ALU.mult).then_inc(s_rsb, 1)
            ve.wait_ge(s_yt, 1 + NT)
            chain = [0]

            def link(ins):
                chain[0] += 1
                ins.then_inc(s_dchain, 1)
                ve.wait_ge(s_dchain, chain[0])

            for g in range(NG):
                link(nc.vector.bn_stats(ON[:, 0, 0, 6 * g:6 * g + 6], Y2[:, 1 + g * GT:1 + (g + 1) * GT]))
            nc.vector.bn_aggr(RST[:, 0:2], ON[:, 0, 0, 0:24]).then_inc(s_gs1, 1)
            ve.wait_ge(s_gs1p, 1)
            link(nc.vector.tensor_copy(RST[:, 2:3], PB[:, 0, 0:1]))
            link(nc.vector.tensor_tensor(RST[:, 3:4], RST[:, 0:1], RST[:, 2:3], ALU.subtract))
            link(nc.vector.tensor_tensor(RST[:, 4:5], RST[:, 3:4], RST[:, 3:4], ALU.mult))
            nc.vector.tensor_tensor(RST[:, 5:6], RST[:, 4:5], RST[:, 1:2], ALU.add).then_inc(s_gs2, 1)
            ve.wait_ge(s_gs2p, 1)
            nc.vector.tensor_copy(RST[:, 9:10], PB[:, 1, 0:1]).then_inc(s_gs4, 1)
            ve.wait_ge(s_gs5, 1)
            link(nc.vector.tensor_tensor(RST[:, 12:13], RST[:, 11:12], GN[:, 0:1], ALU.mult))
            link(nc.vector.tensor_tensor(RST[:, 13:14], RST[:, 12:13], RST[:, 2:3], ALU.mult))
            nc.vector.tensor_tensor(RST[:, 14:15], GN[:, 1:2], RST[:, 13:14], ALU.subtract).then_inc(s_gs6, 1)
            for g in range(NG):
                ve.wait_ge(s_ro, g + 1)
                nc.vector.tensor_tensor(x_group(g), x_group(g), PA[:, g, :], ALU.add).then_inc(s_rox, 1)
            ve.wait_ge(s_rox, NG)
            nc.vector.memset(KT[:, :, GT:GT + WIN], 0.0)
            stack(1)
            ve.wait_ge(s_fin_ps, 1)
            for b in range(4):
                nc.vector.tensor_copy(XNAT.rearrange("p (a b) c -> p a (b c)", a=4)[:, b, :], PA[:, b, :])\
                    .then_inc(s_fin, 1)

        @block.tensor
        def _(pe):
            mm = nc.tensor.matmul

            def attn_group(i, g, L):
                pe.wait_ge(s_wa_in, (L + 1) * 32)
                pe.wait_ge(s_wo_in, (L + 1) * 16)
                pe.wait_ge(s_xg, 2 * (i + 1))
                pe.wait_ge(s_y2, 1 + i)
                for p in range(2 * CH + 2):
                    if p < 2 * CH:
                        b = 2 * (p % 2)
                        pe.wait_ge(s_t2, 1 + i * 16 + (p - 1 if p >= 2 else 0))
                        pe.wait_ge(s_sq, 1 + i * 16 + (p - 1 if p >= 2 else 0))
                        mm(PA[:, b, :], WA[:, p * P:(p + 1) * P], XG[:, :], start=True, stop=True)
                        mm(PA[:, b + 1, :], WA[:, (2 * CH + p) * P:(2 * CH + p + 1) * P], XG[:, :],
                           start=True, stop=True).then_inc(s_pair, 1)
                    if p >= 5 and (p - 5) % 4 == 0:
                        k = (p - 5) // 4
                        pe.wait_ge(s_sq, 1 + i * 16 + 4 * (k + 1))
                        for q in range(4):
                            last = mm(PB[32 * q:32 * q + 32, 2, :], NI[:, k, :], SQ[:, (4 * k + q) % 8, :],
                                      start=(k == 0), stop=(k == 3), tile_position=(0, 32 * q), skip_group_check=True)
                        last.then_inc(s_nb, 1)
                uses = list(order)

                def free_bank(use):
                    k = order.index(use) if use != "v" else len(order) - len(uses)
                    uses.pop(0)
                    if k < 2:
                        return PB[:, k % 2, :]
                    prev = order[k - 2]
                    if prev == "v":
                        pe.wait_ge(s_vev, i * 8 + k - 1)
                    elif prev[0] == "m":
                        pe.wait_ge(s_mt, i * 2 * TPG + 2 * prev[1] + 2)
                    elif prev[0] == "pv":
                        pe.wait_ge(s_on, i * UPG + prev[1] + 1)
                    else:
                        pe.wait_ge(s_ot, i * UPG + prev[1] + 1)
                    return PB[:, k % 2, :]

                for n in range(2 * TPG):
                    t, half = n // 2, n % 2
                    ps = free_bank("v")
                    mm(ps, XG[:, t * P:(t + 1) * P], WA[:, 4 * INNER + half * 512:4 * INNER + (half + 1) * 512],
                       start=True, stop=True).then_inc(s_v, 1)
                pe.wait_ge(s_lo, i + 1)
                pe.wait_ge(s_t2, 1 + i * 16 + 16)
                pe.wait_ge(s_sq, 1 + i * 16 + 16)
                for p in range(2 * CH):
                    if p >= 4:
                        pe.wait_ge(s_qk, i * 16 + p - 3)
                    mm(PA[:, p % 4, :], NO[:, p, :], RHI[:, :], start=True, stop=False)
                    mm(PA[:, p % 4, :], NO[:, p, :], RLO[:, :], start=False, stop=True).then_inc(s_rb, 1)

                def scores(t):
                    pe.wait_ge(s_mx, 1 + i * TPG + t)
                    if t == 0:
                        pe.wait_ge(s_qk, i * 16 + 16)
                    mask = MASKN[:, bass.ds(g, 1), :] if t == 0 else MASKN[:, NG:NG + 1, :]
                    for e in range(2):
                        mm(SN[:, e, :].rearrange("p (c k) -> p c k", c=CH), IDB[:, :],
                           mask.to_broadcast([P, CH, 2 * WIN]),
                           start=True, stop=False, skip_group_check=True)
                    for c in range(CH):
                        for e in range(2):
                            r = slice(64 * e, 64 * e + 64)
                            for w in range(4):
                                a = t * P + w * WIN
                                last = mm(SN[32 * w:32 * w + 32, e, c * 64:(c + 1) * 64],
                                          QT[r, c, a:a + WIN], KT[r, c, a:a + 2 * WIN], start=False,
                                          stop=(c == CH - 1), tile_position=(64 * e, 32 * w), skip_group_check=True)
                    last.then_inc(s_sn, 1)

                def maxima_t(t):
                    ps = free_bank(("m", t)).bitcast(bf16)
                    pe.wait_ge(s_mx, 1 + i * TPG + t + 1)
                    nc.tensor.transpose(ps[0:HEADS, 0:P], NM[:, :], IDB[:, :]).then_inc(s_mtp, 1)

                def scores_t(n):
                    t, u = n // UPT, n % UPT
                    if n >= 2:
                        pe.wait_ge(s_ex, 1 + i * UPG + n - 1)
                    if u == 0:
                        pe.wait_ge(s_mt, i * 2 * TPG + 2 * t + 2)
                    b = 2 * (n % 2)
                    mask = MASKT[:, bass.ds(g, 1), :] if t == 0 else MASKT[:, NG:NG + 1, :]
                    for e in range(2):
                        mm(PA[:, b + e, 0:2 * KCOLS].rearrange("p (c k) -> p c k", c=2), IDB[:, :],
                           mask.to_broadcast([P, 2, KCOLS]), start=True, stop=False, skip_group_check=True)
                    for e in range(2):
                        for cc in range(2):
                            mm(PA[:, b + e, cc * KCOLS:(cc + 1) * KCOLS], SEL[:, e * CH + 2 * u + cc, :], MT[:, :],
                               start=False, stop=False, skip_group_check=True)
                    for cc in range(2):
                        c = 2 * u + cc
                        for e in range(2):
                            r = slice(64 * e, 64 * e + 64)
                            o = cc * KCOLS
                            for w in range(4):
                                a = t * P + w * WIN
                                nq = 2 * WIN if w < 3 else WIN
                                mm(PA[32 * w:32 * w + 32, b + e, o + w * WIN:o + w * WIN + nq],
                                   KT[r, c, WIN + a:2 * WIN + a], QT[r, c, a:a + nq], start=False, stop=False,
                                   tile_position=(64 * e, 32 * w), skip_group_check=True)
                            last = mm(PA[96:128, b + e, o + P:o + KCOLS], KT[r, c, t * P:t * P + WIN],
                                      QT[r, c, t * P:t * P + WIN], start=False, stop=(cc == 1),
                                      tile_position=(64 * e, 96), skip_group_check=True)
                    last.then_inc(s_st, 1)

                def values(n):
                    t, u = n // UPT, n % UPT
                    ps = free_bank(("pv", n))
                    pe.wait_ge(s_ex, 1 + i * UPG + n + 1)
                    if n == 0:
                        pe.wait_ge(s_vev, i * 8 + 8)
                    for h in range(4):
                        s = (h % 2) * 2 + h // 2
                        mm(ps[:, h * VW:(h + 1) * VW], PT[:, n % 2, s, 0:P], VT[:, t + 1, 4 * u + h, :],
                           start=(h == 0), stop=False, skip_group_check=True)
                    for h in range(4):
                        s = (h % 2) * 2 + h // 2
                        last = mm(ps[0:WIN, h * VW:(h + 1) * VW], PT[:, n % 2, s, P:KCOLS], VT[:, t, 4 * u + h, :],
                                  start=False, stop=(h == 3), skip_group_check=True)
                    last.then_inc(s_pv, 1)

                def out_t(n):
                    ps = free_bank(("tr", n))
                    pe.wait_ge(s_on, i * UPG + n + 1)
                    flat = ON[:, n % 2, :, :].rearrange("p h d -> p (h d)")
                    for cc in range(2):
                        last = nc.tensor.transpose(ps[:, cc * P:(cc + 1) * P], flat[:, cc * P:(cc + 1) * P], IDF)
                    last.then_inc(s_tr, 1)

                scores(0)
                maxima_t(0)
                for t in range(TPG):
                    n = UPT * t
                    if t + 1 < TPG:
                        scores(t + 1)
                    scores_t(n)
                    scores_t(n + 1)
                    values(n)
                    if t:
                        out_t(n - 1)
                    scores_t(n + 2)
                    values(n + 1)
                    out_t(n)
                    scores_t(n + 3)
                    values(n + 2)
                    out_t(n + 1)
                    values(n + 3)
                    if t + 1 < TPG:
                        maxima_t(t + 1)
                    out_t(n + 2)
                out_t(UPG - 1)
                pe.wait_ge(s_ot, i * UPG + UPG)
                for c in range(CH):
                    last = mm(SN[:, 1, :], WO[:, c, :], OT[:, c, :], start=(c == 0), stop=(c == CH - 1))
                last.then_inc(s_wo, 1)

            def ffn(L):
                pe.wait_ge(s_xf, (L + 1) * 2 * NG)
                ln_pe(pe, ln_number(L), xf_group)
                pe.wait_ge(s_wf_in, (L + 1) * 48)

                def down(k):
                    g, m = k // 3, k % 3
                    w = HCH[m][1]
                    if m == 0:
                        pe.wait_ge(s_yf, 1 + L * NG + (g - 1 if g >= 2 else 0))
                    pe.wait_ge(s_h, 1 + L * 12 + k + 1)
                    mm(PB[:, g % 2, :], W2[0:w, m, :], HB[0:w, k % 4, :], start=(m == 0), stop=(m == 2))\
                        .then_inc(s_f2, 1)

                for k in range(3 * NG):
                    g, m = k // 3, k % 3
                    lo, w = HCH[m]
                    b = 2 * (k % 2)
                    pe.wait_ge(s_lna, L * NG + g + 1)
                    pe.wait_ge(s_h, 1 + L * 12 + (k - 1 if k >= 2 else 0))
                    mm(PA[0:w, b, :], W1[:, HID + lo:HID + lo + w], xc_group(g), start=True, stop=True)
                    mm(PA[0:w, b + 1, :], W1[:, lo:lo + w], xc_group(g), start=True, stop=True).then_inc(s_f1, 1)
                    if k >= 2:
                        down(k - 2)
                down(3 * NG - 2)
                down(3 * NG - 1)

            def stack(s):
                stack_now[0] = s
                ln_pe(pe, 0 if s == 0 else 8, x_group)
                with pe.Fori(0, DEPTH) as l:
                    L = l + s * DEPTH
                    with pe.Fori(0, NG) as g:
                        attn_group(L * NG + g, g, L)
                    ffn(L)

            pe.wait_ge(s_c_in, 16 * 9)
            pe.wait_ge(s_x_in, 16)
            for t in range(NT):
                last = nc.tensor.transpose(PA[:, t // 4, (t % 4) * P:(t % 4 + 1) * P], XNAT[:, t, :], IDF)
            last.then_inc(s_xt_ps, 1)
            pe.wait_ge(s_xt, 1)
            pe.wait_ge(s_no, 1)
            pe.wait_ge(s_cst, 8)
            stack(0)
            pe.wait_ge(s_xs, NG)
            ln_pe(pe, 7, x_group)
            pe.wait_ge(s_ret_in, 64)
            pe.wait_ge(s_xc, 8 * NG)
            for k in range(4):
                last = nc.tensor.transpose(PA[:, 0, k * P:(k + 1) * P], RW[:, k, :], IDF)
            last.then_inc(s_rwt, 1)
            pe.wait_ge(s_rwe, 1)
            pe.wait_ge(s_lrs, 8 * NG)
            pe.wait_ge(s_rss, 1)
            with pe.Fori(0, NG) as r:
                pe.wait_ge(s_zg, r + 1)
                pe.wait_ge(s_yt, 1 + r * 4)
                mm(PA[:, 0, :], RWT[:, 0, :], ZG, start=True, stop=True)
                mm(PA[:, 1, :], RWT[:, 1, :], ZG, start=True, stop=True).then_inc(s_rq, 1)
                pe.wait_ge(s_rkve, 1 + r)
                for c in range(4):
                    last = mm(PA[:, 2 + c // 2, (c % 2) * 256:(c % 2) * 256 + 256], ZG[:, c * P:(c + 1) * P],
                              RWT[:, 1:3, :], start=True, stop=True)
                last.then_inc(s_rkv, 1)
                pe.wait_ge(s_rqe, 2 * (r + 1))
                for c in range(4):
                    n = r * 4 + c
                    pe.wait_ge(s_qm, n + 1)
                    pe.wait_ge(s_am, 1 + n)
                    for b in range(2):
                        last = mm(PB[:, b, :].rearrange("p (h k) -> p h k", k=P), KR[:, c * P:(c + 1) * P],
                                  QM[:, 4 * b:4 * b + 4, :], start=True, stop=True)
                    last.then_inc(s_ra, 1)
                    if c == 0:
                        pe.wait_ge(s_rqd, r + 1)
                        pe.wait_ge(s_rkd, r + 1)
                    pe.wait_ge(s_rsb, 1 + n)
                    pe.wait_ge(s_yn, 1 + n)
                    mm(PB[:, 2, 0:P], QD[:, c * P:(c + 1) * P], SB, start=True, stop=False, skip_group_check=True)
                    pe.wait_ge(s_am, 1 + n + 1)
                    for h in range(RH):
                        last = mm(PB[:, 2, h * RD:(h + 1) * RD], AM[:, h // 4, (h % 4) * P:(h % 4 + 1) * P],
                                  KV[:, c, P + h * RD:P + (h + 1) * RD], start=False, stop=(h == RH - 1),
                                  skip_group_check=True)
                    last.then_inc(s_ry, 1)
                    mm(PB[:, 3, 0:P], KD[:, c, :], KV[:, c, P:2 * P], start=True, stop=True).then_inc(s_ru, 1)
                    pe.wait_ge(s_yn, 1 + n + 1)
                    nc.tensor.transpose(PA[:, 0, 0:P], YN, IDF).then_inc(s_rtr, 1)
            pe.wait_ge(s_gs1, 1)
            mm(PB[:, 0, 0:1], B16, RST[:, 0:1], start=True, stop=True).then_inc(s_gs1p, 1)
            pe.wait_ge(s_gs2, 1)
            mm(PB[:, 1, 0:1], B16, RST[:, 5:6], start=True, stop=True).then_inc(s_gs2p, 1)
            for g in range(NG):
                pe.wait_ge(s_gy, g + 1)
                mm(PA[:, g, :], RWT[:, 3, :], Y2[:, 1 + g * GT:1 + (g + 1) * GT], start=True, stop=True)\
                    .then_inc(s_ro, 1)
            pe.wait_ge(s_rox, NG)
            stack(1)
            pe.wait_ge(s_xs, 2 * NG)
            for t in range(NT):
                last = nc.tensor.transpose(PA[:, t // 4, (t % 4) * P:(t % 4 + 1) * P], X[:, t * P:(t + 1) * P], IDF)
            last.then_inc(s_fin_ps, 1)


def shape_constants():
    import numpy as np
    f32 = np.float32
    half = np.arange(0, DHEAD, 2, dtype=f32)
    inv_freq = f32(1.0) / np.power(f32(10000.0), half / f32(DHEAD), dtype=f32)
    t = np.arange(NTOK, dtype=f32)
    freqs = (t[:, None] * inv_freq[None, :]).astype(f32)
    base = ((half + f32(0.4 * DHEAD)) / f32(1.4 * DHEAD)).astype(f32)
    power = (t - NTOK // 2) / f32(WIN // 2)
    scale = np.power(base[None, :], power[:, None], dtype=f32)
    cos, sin = np.cos(freqs.astype(np.float64)), np.sin(freqs.astype(np.float64))
    s64 = scale.astype(np.float64)
    ch = np.arange(P) % DHEAD
    d, sign = ch % 32, np.where(ch < 32, -1.0, 1.0)[:, None]
    tables = np.stack([(cos * s64).T[d], (sin * s64).T[d] * sign,
                       (cos / s64).T[d], (sin / s64).T[d] * sign], axis=1).astype(f32)
    norm_in = np.zeros((P, 4, 32), f32)
    norm_out = np.zeros((P, 2 * CH, P), f32)
    for p in range(2 * CH):
        for e in range(2):
            norm_in[64 * e:64 * e + 64, p // 4, 2 * (p // 4) + e] = 1.0
            norm_out[32 * (p % 4) + 2 * (p // 4) + e, p, 64 * e:64 * e + 64] = 1.0
    eye = np.eye(P, dtype=f32)
    blk = (np.arange(P)[:, None] // RD == np.arange(P)[None, :] // RD).astype(f32)
    consts = np.stack([eye, np.full((P, P), 1.0 / P, f32), blk / RD, blk], axis=1).astype(f32)
    big = -1e30
    q = np.arange(P)
    wq, rq = q // WIN, q % WIN
    mask_n = np.zeros((P, 1 + NG, 2 * WIN), f32)
    prev_ok = rq[:, None] <= np.arange(WIN)[None, :]
    own_ok = rq[:, None] >= np.arange(WIN)[None, :]
    mask_n[:, :, 0:WIN] = np.where(prev_ok, 0, big)[:, None, :]
    mask_n[:, :, WIN:] = np.where(own_ok, 0, big)[:, None, :]
    mask_n[0:WIN, 0, 0:WIN] = big
    mask_t = np.full((P, 1 + NG, KCOLS), big, f32)
    dist = q[None, :] - q[:, None]
    ok = (dist >= 0) & (dist <= WIN) & (wq[None, :] - wq[:, None] <= 1)
    mask_t[:, :, 0:P][np.broadcast_to(ok[:, None, :], (P, 1 + NG, P))] = 0
    dist = np.arange(WIN)[None, :] + P - q[:, None]
    ok = (wq[:, None] == 3) & (dist <= WIN)
    mask_t[:, 1:, P:][np.broadcast_to(ok[:, None, :], (P, NG, WIN))] = 0
    sel = np.zeros((P, HEADS + 1, P), f32)
    for h in range(HEADS):
        sel[h, h, :] = 1.0
    sel[:, HEADS, :] = eye
    gam = (f32(1.0) - np.exp(np.linspace(np.log(1.0 / 32.0), np.log(1.0 / 512.0), RH)).astype(f32)).astype(np.float64)
    i = np.arange(P)
    dd = i[None, :] - i[:, None]
    dec_a = np.stack([np.where(dd >= 0, g ** np.maximum(dd, 0), 0.0) for g in gam], axis=1).astype(f32)
    gch = gam[i // RD]
    dq = gch[:, None] ** (i[None, :] + 1)
    dk = gch[None, :] ** (P - 1 - i[:, None])
    hm = np.repeat((np.arange(P)[:, None] // RD == np.arange(RH)[None, :]).astype(f32)[:, :, None], P, axis=2)
    dec_v = np.concatenate([dq[:, None, :], dk[:, None, :], hm], axis=1).astype(f32)
    return tables, norm_in, norm_out, consts, mask_n, mask_t, sel, dec_a, dec_v, (gch ** P).astype(f32)


def kernel(**inputs):
    import numpy as np
    import ml_dtypes
    import concourse.bacc as bacc
    from concourse import mybir as mb
    from concourse.bass_utils import run_bass_kernel_spmd as run

    a = {k: np.ascontiguousarray(v) for k, v in inputs.items()}
    tables, norm_in, norm_out, consts, mask_n, mask_t, sel, dec_a, dec_v, gch = shape_constants()
    bf = ml_dtypes.bfloat16
    wqkv = a["L0_ffn_Wqkv"]
    qk = wqkv[:, :, 0:2 * INNER].reshape(DEPTH, P, 2 * HEADS, 2, DHEAD // 2)
    w_attn = np.concatenate([wqkv[:, :, 0:2 * INNER], qk[:, :, :, ::-1].reshape(DEPTH, P, 2 * INNER),
                             wqkv[:, :, 2 * INNER:]], axis=2)
    w_out = a["L0_ffn_Wo"].reshape(DEPTH, CH, P, P).transpose(0, 2, 1, 3).reshape(DEPTH, P, CH * P)
    qs, ks = a["L0_ffn_q_scale"], a["L0_ffn_k_scale"]
    two = lambda v: np.concatenate([v, v], axis=1)
    swap = lambda v: np.concatenate([v[:, DHEAD // 2:], v[:, :DHEAD // 2]], axis=1)
    prm_attn = np.stack([two(qs), two(swap(qs)), two(ks), two(swap(ks))], axis=2)
    pad = 3 * P - HID
    b1 = a["L0_ffn_b1"]
    cols = lambda v: np.concatenate([v, np.zeros((DEPTH, pad), v.dtype)], axis=1).reshape(DEPTH, 3, P).transpose(0, 2, 1)
    prm_ffn = np.concatenate([a["L0_ffn_ln_g"][:, :, None], a["L0_ffn_ln_b"][:, :, None], cols(b1[:, :HID]),
                              cols(b1[:, HID:]), a["L0_ffn_b2"][:, :, None]], axis=2)
    w2 = np.concatenate([a["L0_ffn_W2"], np.zeros((DEPTH, pad, P), np.float32)], axis=1)
    w2 = w2.reshape(DEPTH, 3, P, P).transpose(0, 2, 1, 3).reshape(DEPTH, P, 3 * P)
    w_ret = np.stack([a["L0_attn_Wq"], a["L0_attn_Wk"], a["L0_attn_Wv"], a["L0_attn_Wo"]], axis=1)
    gn = np.stack([a["L0_attn_gn_weight"], a["L0_attn_gn_bias"], gch], axis=1)
    arrays = dict(x=a["L0_attn_x"], w_attn=w_attn, w_out=w_out, prm_attn=prm_attn, w1=a["L0_ffn_W1"], w2=w2,
                  prm_ffn=prm_ffn, w_ret=w_ret, gn=gn, tables=tables, norm_in=norm_in, norm_out=norm_out,
                  consts=consts, mask_n=mask_n.astype(bf), mask_t=mask_t.astype(bf), sel=sel.astype(bf),
                  dec_a=dec_a, dec_v=dec_v)
    arrays = {k: np.ascontiguousarray(v) for k, v in arrays.items()}
    nc = bacc.Bacc("TRN2", target_bir_lowering=False, num_devices=1)
    aps = {k: nc.dram_tensor("in_" + k, v.shape, mb.dt.from_np(v.dtype), kind="ExternalInput").ap()
           for k, v in arrays.items()}
    out = nc.dram_tensor("out_0", (1, NTOK, P), mb.dt.float32, kind="ExternalOutput").ap()
    build_macaron(nc, out=out, **aps)
    r = run(nc, [{"in_" + k: v for k, v in arrays.items()}], core_ids=[0])
    return r.results[0]["out_0"]
```

```python
import concourse.bass as bass
from concourse import mybir
from contextlib import ExitStack

P = 128
NTOK = 2048
DEPTH = 6
HEADS, DHEAD = 16, 64
INNER = HEADS * DHEAD
WIN = 32
CH = INNER // P
GT = 512
NG = NTOK // GT
TPG = GT // P
NT = NTOK // P
UPT = 4
UPG = UPT * TPG
HID = 341
HCH = [(0, 128), (128, 128), (256, HID - 256)]
VW = DHEAD + 1
KCOLS = P + WIN
RH = 8
RD = P // RH


def build_macaron(nc, x, w_attn, w_out, prm_attn, w1, w2, prm_ffn, w_ret, gn, tables, norm_in,
                  norm_out, consts, mask_n, mask_t, sel, sgn, dec_a, dec_v, out):
    fp32, bf16, f32r = mybir.dt.float32, mybir.dt.bfloat16, mybir.dt.float32r
    ACT, ALU, AX = mybir.ActivationFunctionType, mybir.AluOpType, mybir.AxisListType
    LN_SCALE = 2.0 ** 16
    ctx = ExitStack()
    with ctx:
        def sb(name, shape, dt=fp32):
            return ctx.enter_context(nc.sbuf_tensor(name, shape, dt))

        def sem(name):
            return ctx.enter_context(nc.semaphore(name))

        PA = ctx.enter_context(nc.psum_tensor("PA", [P, 4, 512], fp32))
        PB = ctx.enter_context(nc.psum_tensor("PB", [P, 4, 512], fp32))
        SN = PB[:, 2:4, :]

        X = sb("X", [P, NTOK])
        Y = sb("Y", [P, 1 + NTOK])
        Y2 = sb("Y2", [P, 1 + NTOK])
        TAB = sb("TAB", [P, 4, NTOK])
        WA = sb("WA", [P, 5 * INNER])
        WO = sb("WO", [P, CH, P])
        PRA = sb("PRA", [P, 4])
        W1 = sb("W1", [P, 2 * HID])
        W2 = sb("W2", [P, 3, P])
        PRF = sb("PRF", [P, 9])
        XG = sb("XG", [P, GT])
        T1 = sb("T1", [P, 2, GT])
        T2 = sb("T2", [P, 2, GT])
        SQ = sb("SQ", [P, 8, GT])
        QT = sb("QT", [P, CH, GT])
        KT = sb("KT", [P, CH, WIN + GT])
        NR, LT, RN, RNB = (SQ[:, k, :] for k in range(4))
        RHI = sb("RHI", [P, GT], f32r)
        RSP = sb("RSP", [P, GT], f32r)
        NI = sb("NI", [P, 4, 32])
        NO = sb("NO", [P, 2 * CH, P], f32r)
        VT = sb("VT", [P, 1 + TPG, HEADS, VW])
        PT = sb("PT", [P, 2, 4, KCOLS])
        RC = sb("RC", [P, 2, 4])
        ON = sb("ON", [P, 2, 4, DHEAD])
        OT = sb("OT", [P, CH, GT])
        NMF = sb("NMF", [P, HEADS])
        NM = sb("NM", [P, 2, HEADS], bf16)
        MT = sb("MT", [P, KCOLS], bf16)
        SEL = sb("SEL", [P, HEADS, P], bf16)
        SGN = sb("SGN", [P, 2])
        MASKT = sb("MASKT", [P, 1 + NG, KCOLS], bf16)
        MASKN = sb("MASKN", [P, 1 + NG, 2 * WIN], bf16)
        IDB = sb("IDB", [P, P], bf16)
        CST = sb("CST", [P, 2, P])
        EPS = sb("EPS", [P, 1])
        LNB = sb("LNB", [P, 1])
        RST = sb("RST", [P, 24])
        GN = sb("GN", [P, 3])
        XF = OT[:, 0:4, :]
        XC = OT[:, 4:8, :]
        GE = T1
        HB = SQ[:, 4:8, :]
        XNAT = QT[:, 0:4, :].rearrange("p a (b c) -> p (a b) c", c=P)

        s_c_in = sem("s_c_in")
        s_x_in = sem("s_x_in")
        s_wa_in = sem("s_wa_in")
        s_wo_in = sem("s_wo_in")
        s_wf_in = sem("s_wf_in")
        s_ret_in = sem("s_ret_in")
        s_xt_ps = sem("s_xt_ps")
        s_xt = sem("s_xt")
        s_no = sem("s_no")
        s_cst = sem("s_cst")
        s_xg = sem("s_xg")
        s_vc = sem("s_vc")
        s_kc = sem("s_kc")
        s_pair = sem("s_pair")
        s_t1 = sem("s_t1")
        s_t2 = sem("s_t2")
        s_add = sem("s_add")
        s_sq = sem("s_sq")
        s_nb = sem("s_nb")
        s_nr = sem("s_nr")
        s_ln = sem("s_ln")
        s_rn = sem("s_rn")
        s_hi = sem("s_hi")
        s_lo = sem("s_lo")
        s_v = sem("s_v")
        s_vev = sem("s_vev")
        s_vdv = sem("s_vdv")
        s_rq2 = sem("s_rq2")
        s_rr = sem("s_rr")
        s_rn2 = sem("s_rn2")
        s_rnb = sem("s_rnb")
        s_nmh = sem("s_nmh")
        s_nml = sem("s_nml")
        s_rb = sem("s_rb")
        s_qk = sem("s_qk")
        s_sn = sem("s_sn")
        s_mx = sem("s_mx")
        s_mtp = sem("s_mtp")
        s_mt = sem("s_mt")
        s_st = sem("s_st")
        s_ex = sem("s_ex")
        s_pv = sem("s_pv")
        s_rc = sem("s_rc")
        s_on = sem("s_on")
        s_tr = sem("s_tr")
        s_ot = sem("s_ot")
        s_wo = sem("s_wo")
        s_y2 = sem("s_y2")
        s_mu = sem("s_mu")
        s_xc = sem("s_xc")
        s_lsq = sem("s_lsq")
        s_var = sem("s_var")
        s_lln = sem("s_lln")
        s_lrs = sem("s_lrs")
        s_ldm = sem("s_ldm")
        s_lna = sem("s_lna")
        s_xf = sem("s_xf")
        s_f1 = sem("s_f1")
        s_ge = sem("s_ge")
        s_h = sem("s_h")
        s_f2 = sem("s_f2")
        s_yf = sem("s_yf")
        s_xs = sem("s_xs")
        s_rwt = sem("s_rwt")
        s_rwe = sem("s_rwe")
        s_zg = sem("s_zg")
        s_rq = sem("s_rq")
        s_rqe = sem("s_rqe")
        s_rkv = sem("s_rkv")
        s_rkve = sem("s_rkve")
        s_rqd = sem("s_rqd")
        s_rkd = sem("s_rkd")
        s_qm = sem("s_qm")
        s_ra = sem("s_ra")
        s_am = sem("s_am")
        s_ry = sem("s_ry")
        s_ru = sem("s_ru")
        s_rss = sem("s_rss")
        s_rsb = sem("s_rsb")
        s_yn = sem("s_yn")
        s_yt = sem("s_yt")
        s_rtr = sem("s_rtr")
        s_gs1 = sem("s_gs1")
        s_gs1p = sem("s_gs1p")
        s_gs2 = sem("s_gs2")
        s_gs2p = sem("s_gs2p")
        s_gs4 = sem("s_gs4")
        s_gs5 = sem("s_gs5")
        s_gs6 = sem("s_gs6")
        s_gy = sem("s_gy")
        s_ro = sem("s_ro")
        s_rox = sem("s_rox")
        s_fin_ps = sem("s_fin_ps")
        s_fin = sem("s_fin")
        s_out_done = sem("s_out_done")
        s_dchain = sem("s_dchain")
        s_achain = sem("s_achain")
        block = ctx.enter_context(nc.Block())

        primed = (s_v, s_y2, s_yf, s_pv, s_wo, s_nb, s_t2, s_sq, s_add, s_ex, s_tr, s_h, s_f2, s_mtp, s_mx, s_ra, s_rkv, s_rkve, s_yt, s_am, s_rsb, s_yn)

        IDF, AVG = CST[:, 0, :], CST[:, 1, :]

        RW = QT[:, 0, :].rearrange("p (a n) -> p a n", a=4)
        DA = QT[:, 1:3, :].rearrange("p a (b n) -> p (a b) n", n=P)
        DV = QT[:, 3:6, :].rearrange("p a n -> p (a n)")[:, 0:10 * P].rearrange("p (a n) -> p a n", n=P)
        DQ, DK, HM = DV[:, 0, :], DV[:, 1, :], DV[:, 2:10, :]
        BLK = QT[:, 7, 0:2 * P].rearrange("p (a n) -> p a n", a=2)
        B16, BDG = BLK[:, 0, :], BLK[:, 1, :]
        RWT = QT[:, 6, :].rearrange("p (a n) -> p a n", a=4)
        KR, QR, QD = KT[:, 0, 0:GT], KT[:, 1, 0:GT], KT[:, 2, 0:GT]
        KV = KT[:, 3:6, :].rearrange("p a n -> p (a n)")[:, 0:1024].rearrange("p (a n) -> p a n", a=4)
        KD = KT[:, 6, 0:GT].rearrange("p (a n) -> p a n", a=4)
        ZG = XG[:, :]
        QM = SQ[:, 0:2, :].rearrange("p a (b n) -> p (a b) n", n=P)
        AM = SQ[:, 2:4, :]
        SS, SB, YN = SQ[:, 4, 0:P], SQ[:, 4, P:2 * P], SQ[:, 4, 2 * P:3 * P]

        stack_now = [0]

        def ln_number(L):
            return L + 1 if stack_now[0] == 0 else L + 3

        def v_bank(n):
            return PA[:, n - 2, :] if 2 <= n < 6 else PB[:, n % 2, :]

        order = [("m", 0)]
        for n in range(UPG + 2):
            if n % UPT == UPT - 1 and n // UPT + 1 < TPG:
                order.append(("m", n // UPT + 1))
            if n >= 1 and n <= UPG:
                order.append(("pv", n - 1))
            if n >= 2:
                order.append(("tr", n - 2))
        assert len(order) % 2 == 0

        def bank(use):
            return PB[:, order.index(use) % 2, :]

        @block.sync
        def _(sp):
            sp.dma_start(XNAT, x[0].rearrange("(t p) c -> p t c", p=P)).then_inc(s_x_in, 16)
            sp.dma_start(CST[:, :, :], consts[:, 0:2, :]).then_inc(s_c_in, 16)
            sp.dma_start(NI[:, :, :], norm_in).then_inc(s_c_in, 16)
            sp.dma_start(SQ[:, 0:4, :].rearrange("p a n -> p (a n)"),
                         norm_out.rearrange("p a n -> p (a n)")).then_inc(s_c_in, 16)
            sp.dma_start(GN[:, :], gn).then_inc(s_c_in, 16)
            sp.dma_start(MASKN[:, :, :], mask_n).then_inc(s_c_in, 16)
            sp.dma_start(MASKT[:, :, :], mask_t).then_inc(s_c_in, 16)
            sp.dma_start(SGN[:, :], sgn).then_inc(s_c_in, 16)
            sp.dma_start(SEL[:, :, :], sel[:, 0:HEADS, :]).then_inc(s_c_in, 16)
            sp.dma_start(IDB[:, :], sel[:, HEADS, :]).then_inc(s_c_in, 16)

            def stack_weights(s):
                with sp.Fori(0, DEPTH) as l:
                    L = l + s * DEPTH
                    sp.wait_ge(s_v, 1 + L * (8 * NG))
                    sp.dma_start(WA[:, :], w_attn[bass.ds(l, 1)].rearrange("a p n -> (a p) n")).then_inc(s_wa_in, 16)
                    sp.dma_start(PRA[:, :], prm_attn[bass.ds(l, 1)].rearrange("a p n -> (a p) n")).then_inc(s_wa_in, 16)
                    sp.wait_ge(s_y2, 1 + L * NG)
                    sp.dma_start(WO[:, :, :].rearrange("p a n -> p (a n)"),
                                 w_out[bass.ds(l, 1)].rearrange("a p n -> (a p) n")).then_inc(s_wo_in, 16)
                    sp.wait_ge(s_yf, 1 + L * NG)
                    sp.dma_start(W1[:, :], w1[bass.ds(l, 1)].rearrange("a p n -> (a p) n")).then_inc(s_wf_in, 16)
                    sp.dma_start(W2[:, :, :].rearrange("p a n -> p (a n)"),
                                 w2[bass.ds(l, 1)].rearrange("a p n -> (a p) n")).then_inc(s_wf_in, 16)
                    sp.dma_start(PRF[:, :], prm_ffn[bass.ds(l, 1)].rearrange("a p n -> (a p) n")).then_inc(s_wf_in, 16)

            sp.dma_start(TAB[:, :, :], tables).then_inc(s_c_in, 16)
            stack_weights(0)
            sp.wait_ge(s_y2, 1 + DEPTH * NG)
            sp.wait_ge(s_yf, 1 + DEPTH * NG)
            sp.dma_start(RW[:, :, :], w_ret).then_inc(s_ret_in, 16)
            sp.dma_start(BLK, consts[:, 2:4, :]).then_inc(s_ret_in, 16)
            sp.dma_start(DA[:, :, :], dec_a).then_inc(s_ret_in, 16)
            sp.dma_start(DV[:, :, :], dec_v).then_inc(s_ret_in, 16)
            stack_weights(1)
            sp.wait_ge(s_fin, 4)
            sp.dma_start(out[0].rearrange("(t p) c -> p t c", p=P), XNAT).then_inc(s_out_done, 16)
            sp.wait_ge(s_out_done, 16)

        def ln_pe(pe, n, src, L=None):
            for k in range(NG + 1):
                if k < NG:
                    if L is not None:
                        pe.wait_ge(s_xf, L * 2 * NG + 2 * (k + 1))
                    nc.tensor.matmul(PA[:, k, :], AVG, src(k), start=True, stop=True).then_inc(s_mu, 1)
                if k >= 1:
                    g = k - 1
                    pe.wait_ge(s_lsq, n * NG + g + 1)
                    nc.tensor.matmul(PB[:, g, :], AVG, SQ[:, g, :], start=True, stop=True).then_inc(s_var, 1)

        def ln_dve(ve, n, src, dst, affine):
            for g in range(NG):
                ve.wait_ge(s_mu, n * NG + g + 1)
                nc.vector.tensor_tensor(XC[:, g, :], src(g), PA[:, g, :], ALU.subtract).then_inc(s_xc, 1)
            for k in range(NG + 1):
                if k < NG:
                    ve.wait_ge(s_lrs, n * NG + k + 1)
                    nc.vector.tensor_tensor(dst(k), XC[:, k, :], SQ[:, k, :], ALU.mult).then_inc(s_ldm, 1)
                if k >= 1 and affine is not None:
                    g = k - 1
                    ve.wait_ge(s_ldm, n * NG + g + 1)
                    nc.vector.tensor_scalar(dst(g), dst(g), PRF[:, 0:1], PRF[:, 1:2], ALU.mult, ALU.add)\
                        .then_inc(s_lna, 1)

        def ln_act(ac, n):
            for k in range(NG + 1):
                if k < NG:
                    ac.wait_ge(s_xc, n * NG + k + 1)
                    nc.scalar.activation(SQ[:, k, :], XC[:, k, :], ACT.Square).then_inc(s_lsq, 1)
                if k >= 1:
                    g = k - 1
                    ac.wait_ge(s_var, n * NG + g + 1)
                    nc.scalar.activation(SQ[:, g, :], PB[:, g, :], ACT.Ln, bias=EPS[:, 0:1]).then_inc(s_lln, 1)
                    ac.wait_ge(s_lln, n * NG + g + 1)
                    nc.scalar.activation(SQ[:, g, :], SQ[:, g, :], ACT.Exp, scale=-0.5).then_inc(s_lrs, 1)

        def x_group(g):
            return X[:, g * GT:(g + 1) * GT]

        def y_group(g):
            return Y[:, 1 + g * GT:1 + (g + 1) * GT]

        def xf_group(g):
            return XF[:, g, :]

        def xc_group(g):
            return XC[:, g, :]

        @block.gpsimd
        def _(po):
            for started in primed:
                po.sem_inc(started, 1)
            po.memset(Y[:, 0:1], 0.0).then_inc(s_cst, 1)
            po.memset(Y2[:, 0:1], 0.0).then_inc(s_cst, 1)
            po.memset(KT[:, :, :], 0.0).then_inc(s_cst, 1)
            po.memset(VT[:, :, :, 0:DHEAD], 0.0).then_inc(s_cst, 1)
            po.memset(VT[:, :, :, DHEAD:VW], 1.0).then_inc(s_cst, 1)
            po.memset(MT[:, :], 0.0).then_inc(s_cst, 1)
            po.memset(EPS[:, :], 1e-5).then_inc(s_cst, 1)
            po.memset(LNB[:, :], 8.0 * 0.6931471805599453).then_inc(s_cst, 1)

            def attn_group(i):
                for p in range(2 * CH):
                    if p == CH:
                        po.wait_ge(s_kc, i + 1)
                    po.wait_ge(s_t2, 1 + i * 16 + p + 1)
                    dst = QT[:, p, :] if p < CH else KT[:, p - CH, WIN:WIN + GT]
                    po.tensor_tensor(dst, T1[:, p % 2, :], T2[:, p % 2, :], ALU.add).then_inc(s_add, 1)

            for s in range(2):
                with po.Fori(0, DEPTH) as l:
                    with po.Fori(0, NG) as g:
                        attn_group((l + s * DEPTH) * NG + g)

        @block.scalar
        def _(ac):
            def attn_group(i, g, L):
                ac.wait_ge(s_yf, 1 + L * NG)
                ac.wait_ge(s_v, 1 + i * 8)
                for lo, back in ((0, 0), (64, 1)):
                    nc.scalar.activation(XG[lo:lo + 64, :], Y[lo:lo + 64, bass.ds(g * GT + 1 - back, GT)],
                                         ACT.Copy).then_inc(s_xg, 1)
                ac.wait_ge(s_pv, 1 + i * UPG)
                nc.scalar.activation(VT[:, 0, :, 0:DHEAD], VT[:, TPG, :, 0:DHEAD], ACT.Copy).then_inc(s_vc, 1)
                nc.scalar.activation(KT[:, :, 0:WIN], KT[:, :, GT:GT + WIN], ACT.Copy).then_inc(s_kc, 1)
                for p in range(2 * CH):
                    ac.wait_ge(s_t1, i * 16 + p + 1)
                    ac.wait_ge(s_nb, 1 + i * 4 + ((p - 8) // 4 + 1 if p >= 8 else 0))
                    nc.scalar.activation(SQ[:, p % 8, :], PA[:, 2 * (p % 2), :], ACT.Square).then_inc(s_sq, 1)
                ac.wait_ge(s_vc, i + 1)

                def values_copy(n):
                    t, half = n // 2, n % 2
                    ac.wait_ge(s_v, 1 + i * 8 + n + 1)
                    nc.scalar.activation(VT[:, t + 1, 8 * half:8 * half + 8, 0:DHEAD],
                                         v_bank(n).rearrange("p (h d) -> p h d", d=DHEAD),
                                         ACT.Copy).then_inc(s_vev, 1)

                values_copy(0)
                values_copy(1)
                ac.wait_ge(s_nr, i + 1)
                nc.scalar.activation(LT, NR, ACT.Ln, scale=LN_SCALE).then_inc(s_ln, 1)
                ac.wait_ge(s_ln, i + 1)
                nc.scalar.activation(RN, LT, ACT.Exp, scale=-0.5, bias=LNB[:, 0:1]).then_inc(s_rn, 1)
                values_copy(4)
                values_copy(5)
                ac.wait_ge(s_rn2, i + 1)
                nc.scalar.activation(RNB, RN, ACT.Copy, scale=SGN[:, 1:2]).then_inc(s_rnb, 1)
                values_copy(6)
                values_copy(7)

                def exps(n):
                    ac.wait_ge(s_st, i * UPG + n + 1)
                    ac.wait_ge(s_pv, 1 + i * UPG + (n - 1 if n >= 2 else 0))
                    b = n % 2
                    nc.scalar.activation(PT[:, b, :, :].rearrange("p (e c) n -> p e (c n)", e=2),
                                         PA[:, 2 * b:2 * b + 2, 0:2 * KCOLS], ACT.Exp, scale=8.0).then_inc(s_ex, 1)

                def out_copy(n):
                    t, u = n // UPT, n % UPT
                    ac.wait_ge(s_tr, 1 + i * UPG + n + 1)
                    nc.scalar.activation(OT[:, 2 * u:2 * u + 2, t * P:(t + 1) * P],
                                         bank(("tr", n))[:, 0:2 * P].rearrange("p (c n) -> p c n", c=2),
                                         ACT.Copy).then_inc(s_ot, 1)

                ac.wait_ge(s_wo, 1 + i)
                for n in range(UPG):
                    exps(n)
                    if n >= 2:
                        out_copy(n - 2)
                out_copy(UPG - 2)
                out_copy(UPG - 1)

            def ffn(L):
                ln_act(ac, ln_number(L))
                for k in range(3 * NG):
                    g, m = k // 3, k % 3
                    w = HCH[m][1]
                    ac.wait_ge(s_f1, L * 12 + k + 1)
                    ac.wait_ge(s_h, 1 + L * 12 + k - 1 if k >= 2 else L * 12)
                    nc.scalar.activation(GE[0:w, k % 2, :], PA[0:w, 2 * (k % 2), :], ACT.Gelu,
                                         bias=PRF[0:w, 5 + m:6 + m]).then_inc(s_ge, 1)
                ac.preload_act_table_set("natural_log_exp_and_others")

            def stack(s):
                stack_now[0] = s
                ln_act(ac, 0 if s == 0 else 8)
                ac.wait_ge(s_ldm, NG * (1 if s == 0 else 9))
                ac.preload_act_table_set("natural_log_exp_and_others")
                with ac.Fori(0, DEPTH) as l:
                    L = l + s * DEPTH
                    with ac.Fori(0, NG) as g:
                        attn_group(L * NG + g, g, L)
                    ffn(L)

            ac.wait_ge(s_cst, 8)
            stack(0)
            ln_act(ac, 7)
            ac.wait_ge(s_rwt, 1)
            nc.scalar.activation(RWT, PA[:, 0, :].rearrange("p (a n) -> p a n", a=4), ACT.Copy).then_inc(s_rwe, 1)
            ac.wait_ge(s_ldm, NG * 8)
            with ac.Fori(0, NG) as r:
                ac.wait_ge(s_rkv, 1 + r)
                nc.scalar.activation(ZG, Y[:, bass.ds(r * GT + 1, GT)], ACT.Copy).then_inc(s_zg, 1)
                ac.wait_ge(s_rq, r + 1)
                ac.wait_ge(s_ra, 1 + r * 4)
                nc.scalar.activation(KR, PA[:, 1, :], ACT.Copy).then_inc(s_rqe, 1)
                nc.scalar.activation(QR, PA[:, 0, :], ACT.Copy).then_inc(s_rqe, 1)
                ac.wait_ge(s_rkv, 1 + r + 1)
                nc.scalar.activation(KV.rearrange("p (b a) n -> p b (a n)", b=2), PA[:, 2:4, :],
                                     ACT.Copy).then_inc(s_rkve, 1)
                for c in range(4):
                    ac.wait_ge(s_ry, r * 4 + c + 1)
                    nc.scalar.activation(YN, PB[:, 2, 0:P], ACT.Copy).then_inc(s_yn, 1)
                    ac.wait_ge(s_rtr, r * 4 + c + 1)
                    nc.scalar.activation(Y2[:, bass.ds(r * GT + 1 + c * P, P)], PA[:, 0, 0:P],
                                         ACT.Copy).then_inc(s_yt, 1)
            ac.wait_ge(s_gs4, 1)
            nc.scalar.activation(RST[:, 10:11], RST[:, 9:10], ACT.Ln, bias=EPS[:, 0:1]).then_inc(s_achain, 1)
            ac.wait_ge(s_achain, 1)
            nc.scalar.activation(RST[:, 11:12], RST[:, 10:11], ACT.Exp, scale=-0.5).then_inc(s_gs5, 1)
            ac.wait_ge(s_gs6, 1)
            for g in range(NG):
                nc.scalar.activation(Y2[:, 1 + g * GT:1 + (g + 1) * GT], Y2[:, 1 + g * GT:1 + (g + 1) * GT],
                                     ACT.Identity, scale=RST[:, 12:13], bias=RST[:, 14:15]).then_inc(s_gy, 1)
            stack(1)

        @block.vector
        def _(ve):
            def attn_group(i, g, L):
                ve.wait_ge(s_wa_in, (L + 1) * 32)
                for p in range(2 * CH):
                    kind, b = p // CH, 2 * (p % 2)
                    ve.wait_ge(s_pair, i * 16 + p + 1)
                    ve.wait_ge(s_add, 1 + i * 16 + (p - 1 if p >= 2 else 0))
                    nc.vector.scalar_tensor_tensor(
                        out=T1[:, p % 2, :], in0=PA[:, b, :], scalar=PRA[:, 2 * kind:2 * kind + 1],
                        in1=TAB[:, 2 * kind, bass.ds(g * GT, GT)], op0=ALU.mult, op1=ALU.mult).then_inc(s_t1, 1)
                    nc.vector.scalar_tensor_tensor(
                        out=T2[:, p % 2, :], in0=PA[:, b + 1, :], scalar=PRA[:, 2 * kind + 1:2 * kind + 2],
                        in1=TAB[:, 2 * kind + 1, bass.ds(g * GT, GT)], op0=ALU.mult, op1=ALU.mult).then_inc(s_t2, 1)
                ve.wait_ge(s_nb, 1 + i * 4 + 4)
                nc.vector.tensor_scalar_max(NR, SN[:, 0, :], 1e-24).then_inc(s_nr, 1)

                def values_copy(n):
                    t, half = n // 2, n % 2
                    ve.wait_ge(s_v, 1 + i * 8 + n + 1)
                    nc.vector.tensor_copy(VT[:, t + 1, 8 * half:8 * half + 8, 0:DHEAD],
                                          v_bank(n).rearrange("p (h d) -> p h d", d=DHEAD)).then_inc(s_vdv, 1)

                values_copy(2)
                values_copy(3)
                ve.wait_ge(s_rn, i + 1)
                nc.vector.tensor_tensor(LT, RN, RN, ALU.mult).then_inc(s_rq2, 1)
                ve.wait_ge(s_rq2, i + 1)
                nc.vector.scalar_tensor_tensor(out=LT, in0=LT, scalar=-0.5, in1=NR, op0=ALU.mult,
                                               op1=ALU.mult).then_inc(s_rr, 1)
                ve.wait_ge(s_rr, i + 1)
                nc.vector.scalar_tensor_tensor(out=RN, in0=LT, scalar=1.5, in1=RN, op0=ALU.add,
                                               op1=ALU.mult).then_inc(s_rn2, 1)
                ve.wait_ge(s_rn2, i + 1)
                nc.vector.tensor_copy(RHI[:, :], RN).then_inc(s_hi, 1)
                ve.wait_ge(s_hi, i + 1)
                ve.wait_ge(s_rnb, i + 1)
                nc.vector.scalar_tensor_tensor(out=RSP[:, :], in0=RHI[:, :].bitcast(fp32), scalar=SGN[:, 0:1], in1=RNB,
                                               op0=ALU.mult, op1=ALU.add).then_inc(s_lo, 1)
                for k in range(2 * CH):
                    c, kind = k // 2, k % 2
                    ve.wait_ge(s_rb, i * 16 + k + 1)
                    ve.wait_ge(s_add, 1 + i * 16 + 16)
                    dst = QT[:, c, :] if kind == 0 else KT[:, c, WIN:WIN + GT]
                    nc.vector.tensor_tensor(dst, dst, PA[:, k % 4, :], ALU.mult).then_inc(s_qk, 1)

                def maxima(t):
                    ve.wait_ge(s_sn, i * TPG + t + 1)
                    ve.wait_ge(s_mtp, 1 + i * TPG + t)
                    nc.vector.tensor_reduce(NMF[:, :], SN.rearrange("p e (c k) -> p (e c) k", k=2 * WIN),
                                            AX.X, ALU.max, negate=True).then_inc(s_mx, 1)
                    ve.wait_ge(s_mx, 1 + i * TPG + t + 1)
                    nc.vector.tensor_copy(NM[:, 0, :], NMF[:, :]).then_inc(s_nmh, 1)
                    ve.wait_ge(s_nmh, i * TPG + t + 1)
                    nc.vector.tensor_tensor(NM[:, 1, :], NMF[:, :], NM[:, 0, :], ALU.subtract).then_inc(s_nml, 1)

                def maxima_copy(t):
                    ve.wait_ge(s_mtp, 1 + i * TPG + t + 1)
                    ps = bank(("m", t)).bitcast(bf16)
                    nc.vector.tensor_copy(MT[0:2 * HEADS, 0:P], ps[0:2 * HEADS, 0:P]).then_inc(s_mt, 1)
                    nc.vector.tensor_copy(MT[0:2 * HEADS, P:KCOLS], ps[0:2 * HEADS, 0:WIN]).then_inc(s_mt, 1)

                def normalise(n):
                    ve.wait_ge(s_pv, 1 + i * UPG + n + 1)
                    ve.wait_ge(s_tr, 1 + i * UPG + (n - 1 if n >= 2 else 0))
                    ps = bank(("pv", n))[:, 0:4 * VW].rearrange("p (h d) -> p h d", d=VW)
                    nc.vector.reciprocal(RC[:, n % 2, :].unsqueeze(2), ps[:, :, DHEAD:VW]).then_inc(s_rc, 1)
                    ve.wait_ge(s_rc, i * UPG + n + 1)
                    nc.vector.tensor_tensor(ON[:, n % 2, :, :], ps[:, :, 0:DHEAD],
                                            RC[:, n % 2, :].unsqueeze(2).to_broadcast([P, 4, DHEAD]),
                                            ALU.mult).then_inc(s_on, 1)

                maxima(0)
                maxima_copy(0)
                for n in range(UPG + 1):
                    if n % UPT == 1 and n // UPT + 1 < TPG:
                        maxima(n // UPT + 1)
                    if n % UPT == UPT - 1 and n // UPT + 1 < TPG:
                        maxima_copy(n // UPT + 1)
                    if n >= 1:
                        normalise(n - 1)
                ve.wait_ge(s_wo, 1 + i + 1)
                nc.vector.tensor_tensor(Y2[:, bass.ds(g * GT + 1, GT)], SN[:, 1, :],
                                        Y[:, bass.ds(g * GT + 1, GT)], ALU.add).then_inc(s_y2, 1)

            def ffn(L):
                ve.wait_ge(s_y2, 1 + (L + 1) * NG)
                nc.vector.memset(KT[:, :, GT:GT + WIN], 0.0)
                for g in range(NG):
                    for lo, back in ((0, 0), (64, 1)):
                        a = g * GT + 1 - back
                        nc.vector.tensor_copy(XF[lo:lo + 64, g, :], Y2[lo:lo + 64, a:a + GT]).then_inc(s_xf, 1)
                ve.wait_ge(s_xf, (L + 1) * 2 * NG)
                ve.wait_ge(s_wf_in, (L + 1) * 48)
                ln_dve(ve, ln_number(L), xf_group, xc_group, True)

                def residual(g):
                    ve.wait_ge(s_f2, 1 + L * 12 + 3 * g + 3)
                    nc.vector.scalar_tensor_tensor(out=y_group(g), in0=PB[:, g % 2, :], scalar=PRF[:, 8:9],
                                                   in1=Y2[:, 1 + g * GT:1 + (g + 1) * GT],
                                                   op0=ALU.add, op1=ALU.add).then_inc(s_yf, 1)

                for k in range(3 * NG):
                    m = k % 3
                    w = HCH[m][1]
                    ve.wait_ge(s_ge, L * 12 + k + 1)
                    ve.wait_ge(s_f2, 1 + L * 12 + (k - 3 if k >= 4 else 0))
                    nc.vector.scalar_tensor_tensor(out=HB[0:w, k % 4, :], in0=PA[0:w, 2 * (k % 2) + 1, :],
                                                   scalar=PRF[0:w, 2 + m:3 + m], in1=GE[0:w, k % 2, :],
                                                   op0=ALU.add, op1=ALU.mult).then_inc(s_h, 1)
                    if k >= 5 and (k - 5) % 3 == 0:
                        residual((k - 5) // 3)
                residual(NG - 1)

            def stack(s):
                stack_now[0] = s
                ln_dve(ve, 0 if s == 0 else 8, x_group, y_group, None)
                with ve.Fori(0, DEPTH) as l:
                    L = l + s * DEPTH
                    with ve.Fori(0, NG) as g:
                        attn_group(L * NG + g, g, L)
                    ffn(L)
                for g in range(NG):
                    ve.wait_ge(s_yf, 1 + (s + 1) * DEPTH * NG)
                    nc.vector.scalar_tensor_tensor(out=x_group(g), in0=y_group(g), scalar=0.5, in1=x_group(g),
                                                   op0=ALU.mult, op1=ALU.add).then_inc(s_xs, 1)

            ve.wait_ge(s_c_in, 16 * 10)
            nc.vector.tensor_copy(NO[:, :, :], SQ[:, 0:4, :].rearrange("p a (b n) -> p (a b) n", n=P)).then_inc(s_no, 1)
            ve.wait_ge(s_xt_ps, 1)
            nc.vector.tensor_copy(X[:, :], PA[:, :, :].rearrange("p a n -> p (a n)")).then_inc(s_xt, 1)
            ve.wait_ge(s_xt, 1)
            ve.wait_ge(s_cst, 8)
            stack(0)
            ve.wait_ge(s_xs, NG)
            ln_dve(ve, 7, x_group, y_group, None)
            nc.vector.memset(SQ[:, 4, 0:2 * P], 0.0).then_inc(s_rss, 1)
            ve.wait_ge(s_ret_in, 64)
            with ve.Fori(0, NG) as r:
                ve.wait_ge(s_rqe, 2 * (r + 1))
                nc.vector.tensor_tensor(QD.rearrange("p (a n) -> p a n", a=4), QR.rearrange("p (a n) -> p a n", a=4),
                                        DQ.unsqueeze(1).to_broadcast([P, 4, P]), ALU.mult).then_inc(s_rqd, 1)
                ve.wait_ge(s_rkve, 1 + r + 1)
                nc.vector.tensor_tensor(KD, KV[:, :, 0:P], DK.unsqueeze(1).to_broadcast([P, 4, P]),
                                        ALU.mult).then_inc(s_rkd, 1)
                for c in range(4):
                    n = r * 4 + c
                    ve.wait_ge(s_ra, 1 + n)
                    nc.vector.tensor_tensor(QM, QR[:, c * P:(c + 1) * P].unsqueeze(1).to_broadcast([P, RH, P]), HM,
                                            ALU.mult).then_inc(s_qm, 1)
                    ve.wait_ge(s_ra, 1 + n + 1)
                    nc.vector.tensor_tensor(AM, PB[:, 0:2, :], DA.rearrange("p (b a) n -> p b (a n)", b=2),
                                            ALU.mult).then_inc(s_am, 1)
                    ve.wait_ge(s_ru, n + 1)
                    ve.wait_ge(s_rss, n + 1)
                    nc.vector.scalar_tensor_tensor(out=SS, in0=SS, scalar=GN[:, 2:3], in1=PB[:, 3, 0:P],
                                                   op0=ALU.mult, op1=ALU.add).then_inc(s_rss, 1)
                    ve.wait_ge(s_rss, n + 2)
                    nc.vector.tensor_tensor(SB, SS, BDG, ALU.mult).then_inc(s_rsb, 1)
            ve.wait_ge(s_yt, 1 + NT)
            chain = [0]

            def link(ins):
                chain[0] += 1
                ins.then_inc(s_dchain, 1)
                ve.wait_ge(s_dchain, chain[0])

            for g in range(NG):
                link(nc.vector.bn_stats(ON[:, 0, 0, 6 * g:6 * g + 6], Y2[:, 1 + g * GT:1 + (g + 1) * GT]))
            nc.vector.bn_aggr(RST[:, 0:2], ON[:, 0, 0, 0:24]).then_inc(s_gs1, 1)
            ve.wait_ge(s_gs1p, 1)
            link(nc.vector.tensor_copy(RST[:, 2:3], PB[:, 0, 0:1]))
            link(nc.vector.tensor_tensor(RST[:, 3:4], RST[:, 0:1], RST[:, 2:3], ALU.subtract))
            link(nc.vector.tensor_tensor(RST[:, 4:5], RST[:, 3:4], RST[:, 3:4], ALU.mult))
            nc.vector.tensor_tensor(RST[:, 5:6], RST[:, 4:5], RST[:, 1:2], ALU.add).then_inc(s_gs2, 1)
            ve.wait_ge(s_gs2p, 1)
            nc.vector.tensor_copy(RST[:, 9:10], PB[:, 1, 0:1]).then_inc(s_gs4, 1)
            ve.wait_ge(s_gs5, 1)
            link(nc.vector.tensor_tensor(RST[:, 12:13], RST[:, 11:12], GN[:, 0:1], ALU.mult))
            link(nc.vector.tensor_tensor(RST[:, 13:14], RST[:, 12:13], RST[:, 2:3], ALU.mult))
            nc.vector.tensor_tensor(RST[:, 14:15], GN[:, 1:2], RST[:, 13:14], ALU.subtract).then_inc(s_gs6, 1)
            for g in range(NG):
                ve.wait_ge(s_ro, g + 1)
                nc.vector.tensor_tensor(x_group(g), x_group(g), PA[:, g, :], ALU.add).then_inc(s_rox, 1)
            ve.wait_ge(s_rox, NG)
            nc.vector.memset(KT[:, :, GT:GT + WIN], 0.0)
            stack(1)
            ve.wait_ge(s_fin_ps, 1)
            for b in range(4):
                nc.vector.tensor_copy(XNAT.rearrange("p (a b) c -> p a (b c)", a=4)[:, b, :], PA[:, b, :])\
                    .then_inc(s_fin, 1)

        @block.tensor
        def _(pe):
            mm = nc.tensor.matmul

            def attn_group(i, g, L):
                pe.wait_ge(s_wa_in, (L + 1) * 32)
                pe.wait_ge(s_wo_in, (L + 1) * 16)
                pe.wait_ge(s_xg, 2 * (i + 1))
                pe.wait_ge(s_y2, 1 + i)
                def norms(k):
                    pe.wait_ge(s_sq, 1 + i * 16 + 4 * (k + 1))
                    for q in range(4):
                        last = mm(PB[32 * q:32 * q + 32, 2, :], NI[:, k, :], SQ[:, (4 * k + q) % 8, :],
                                  start=(k == 0), stop=(k == 3), tile_position=(0, 32 * q), skip_group_check=True)
                    last.then_inc(s_nb, 1)

                for p in range(2 * CH):
                    b = 2 * (p % 2)
                    pe.wait_ge(s_t2, 1 + i * 16 + (p - 1 if p >= 2 else 0))
                    pe.wait_ge(s_sq, 1 + i * 16 + (p - 1 if p >= 2 else 0))
                    mm(PA[:, b, :], WA[:, p * P:(p + 1) * P], XG[:, :], start=True, stop=True)
                    mm(PA[:, b + 1, :], WA[:, (2 * CH + p) * P:(2 * CH + p + 1) * P], XG[:, :],
                       start=True, stop=True).then_inc(s_pair, 1)
                    if p >= 5 and (p - 5) % 4 == 0:
                        norms((p - 5) // 4)

                def free_bank(use):
                    k = order.index(use)
                    if k < 2:
                        pe.wait_ge(s_vev, i * 6 + 5 + k)
                        return PB[:, k % 2, :]
                    prev = order[k - 2]
                    if prev[0] == "m":
                        pe.wait_ge(s_mt, i * 2 * TPG + 2 * prev[1] + 2)
                    elif prev[0] == "pv":
                        pe.wait_ge(s_on, i * UPG + prev[1] + 1)
                    else:
                        pe.wait_ge(s_ot, i * UPG + prev[1] + 1)
                    return PB[:, k % 2, :]

                def values_in(n):
                    t, half = n // 2, n % 2
                    if n == 2:
                        norms(3)
                        pe.wait_ge(s_t2, 1 + i * 16 + 16)
                    if n >= 6:
                        pe.wait_ge(s_vev, i * 6 + n - 5)
                        pe.wait_ge(s_qk, i * 16 + 2 * n + 2)
                    mm(v_bank(n), XG[:, t * P:(t + 1) * P],
                       WA[:, 4 * INNER + half * 512:4 * INNER + (half + 1) * 512],
                       start=True, stop=True).then_inc(s_v, 1)

                for n in range(6):
                    values_in(n)

                def scores_mask(t):
                    mask = MASKN[:, bass.ds(g, 1), :] if t == 0 else MASKN[:, NG:NG + 1, :]
                    for e in range(2):
                        mm(SN[:, e, :].rearrange("p (c k) -> p c k", c=CH), IDB[:, :],
                           mask.to_broadcast([P, CH, 2 * WIN]),
                           start=True, stop=False, skip_group_check=True)

                def scores_chunk(t, c):
                    for e in range(2):
                        r = slice(64 * e, 64 * e + 64)
                        for w in range(4):
                            a = t * P + w * WIN
                            last = mm(SN[32 * w:32 * w + 32, e, c * 64:(c + 1) * 64],
                                      QT[r, c, a:a + WIN], KT[r, c, a:a + 2 * WIN], start=False,
                                      stop=(c == CH - 1), tile_position=(64 * e, 32 * w), skip_group_check=True)
                    if c == CH - 1:
                        last.then_inc(s_sn, 1)

                def scores(t):
                    pe.wait_ge(s_mx, 1 + i * TPG + t)
                    scores_mask(t)
                    for c in range(CH):
                        scores_chunk(t, c)

                pe.wait_ge(s_lo, i + 1)
                pe.wait_ge(s_mx, 1 + i * TPG)
                for k in range(2 * CH + 4):
                    if k < 2 * CH:
                        c, kind = k // 2, k % 2
                        if k < 2:
                            pe.wait_ge(s_vdv, i * 2 + k + 1)
                        elif k < 4:
                            pe.wait_ge(s_vev, i * 6 + 1 + k)
                        else:
                            pe.wait_ge(s_qk, i * 16 + k - 3)
                        mm(PA[:, k % 4, :], NO[:, kind * CH + c, :], RSP[:, :], start=True, stop=True).then_inc(s_rb, 1)
                        if k == 3:
                            scores_mask(0)
                    if k >= 5 and k % 2:
                        if k >= 2 * CH:
                            values_in(6 + (k - 2 * CH) // 2)
                        scores_chunk(0, (k - 5) // 2)

                def maxima_t(t):
                    ps = free_bank(("m", t)).bitcast(bf16)
                    pe.wait_ge(s_nml, i * TPG + t + 1)
                    nc.tensor.transpose(ps[0:2 * HEADS, 0:P], NM[:, :, :].rearrange("p a h -> p (a h)"), IDB[:, :])\
                        .then_inc(s_mtp, 1)

                def scores_t(n):
                    t, u = n // UPT, n % UPT
                    if n >= 2:
                        pe.wait_ge(s_ex, 1 + i * UPG + n - 1)
                    else:
                        pe.wait_ge(s_qk, i * 16 + 16)
                    if u == 0:
                        pe.wait_ge(s_mt, i * 2 * TPG + 2 * t + 2)
                    b = 2 * (n % 2)
                    mask = MASKT[:, bass.ds(g, 1), :] if t == 0 else MASKT[:, NG:NG + 1, :]
                    for e in range(2):
                        mm(PA[:, b + e, 0:2 * KCOLS].rearrange("p (c k) -> p c k", c=2), IDB[:, :],
                           mask.to_broadcast([P, 2, KCOLS]), start=True, stop=False, skip_group_check=True)
                    for e in range(2):
                        for cc in range(2):
                            mm(PA[:, b + e, cc * KCOLS:(cc + 1) * KCOLS], SEL[:, e * CH + 2 * u + cc, :], MT[:, :],
                               start=False, stop=False, skip_group_check=True)
                    for cc in range(2):
                        c = 2 * u + cc
                        for e in range(2):
                            r = slice(64 * e, 64 * e + 64)
                            o = cc * KCOLS
                            for w in range(4):
                                a = t * P + w * WIN
                                nq = 2 * WIN if w < 3 else WIN
                                mm(PA[32 * w:32 * w + 32, b + e, o + w * WIN:o + w * WIN + nq],
                                   KT[r, c, WIN + a:2 * WIN + a], QT[r, c, a:a + nq], start=False, stop=False,
                                   tile_position=(64 * e, 32 * w), skip_group_check=True)
                            last = mm(PA[96:128, b + e, o + P:o + KCOLS], KT[r, c, t * P:t * P + WIN],
                                      QT[r, c, t * P:t * P + WIN], start=False, stop=(cc == 1),
                                      tile_position=(64 * e, 96), skip_group_check=True)
                    last.then_inc(s_st, 1)

                def values(n):
                    t, u = n // UPT, n % UPT
                    ps = free_bank(("pv", n))
                    pe.wait_ge(s_ex, 1 + i * UPG + n + 1)
                    if n == 0:
                        pe.wait_ge(s_vdv, i * 2 + 2)
                        pe.wait_ge(s_vev, i * 6 + 6)
                    for h in range(4):
                        s = (h % 2) * 2 + h // 2
                        mm(ps[:, h * VW:(h + 1) * VW], PT[:, n % 2, s, 0:P], VT[:, t + 1, 4 * u + h, :],
                           start=(h == 0), stop=False, skip_group_check=True)
                    for h in range(4):
                        s = (h % 2) * 2 + h // 2
                        last = mm(ps[0:WIN, h * VW:(h + 1) * VW], PT[:, n % 2, s, P:KCOLS], VT[:, t, 4 * u + h, :],
                                  start=False, stop=(h == 3), skip_group_check=True)
                    last.then_inc(s_pv, 1)

                def out_t(n):
                    ps = free_bank(("tr", n))
                    pe.wait_ge(s_on, i * UPG + n + 1)
                    flat = ON[:, n % 2, :, :].rearrange("p h d -> p (h d)")
                    for cc in range(2):
                        last = nc.tensor.transpose(ps[:, cc * P:(cc + 1) * P], flat[:, cc * P:(cc + 1) * P], IDF)
                    last.then_inc(s_tr, 1)

                maxima_t(0)
                for n in range(UPG + 2):
                    if n % UPT == 1 and n // UPT + 1 < TPG:
                        scores(n // UPT + 1)
                    if n < UPG:
                        scores_t(n)
                    if n % UPT == UPT - 1 and n // UPT + 1 < TPG:
                        maxima_t(n // UPT + 1)
                    if 1 <= n <= UPG:
                        values(n - 1)
                    if n >= 2:
                        out_t(n - 2)
                pe.wait_ge(s_ot, i * UPG + UPG)
                for c in range(CH):
                    last = mm(SN[:, 1, :], WO[:, c, :], OT[:, c, :], start=(c == 0), stop=(c == CH - 1))
                last.then_inc(s_wo, 1)

            def ffn(L):
                ln_pe(pe, ln_number(L), xf_group, L)
                pe.wait_ge(s_wf_in, (L + 1) * 48)

                def down(k):
                    g, m = k // 3, k % 3
                    w = HCH[m][1]
                    if m == 0:
                        pe.wait_ge(s_yf, 1 + L * NG + (g - 1 if g >= 2 else 0))
                    pe.wait_ge(s_h, 1 + L * 12 + k + 1)
                    mm(PB[:, g % 2, :], W2[0:w, m, :], HB[0:w, k % 4, :], start=(m == 0), stop=(m == 2))\
                        .then_inc(s_f2, 1)

                for k in range(3 * NG):
                    g, m = k // 3, k % 3
                    lo, w = HCH[m]
                    b = 2 * (k % 2)
                    pe.wait_ge(s_lna, L * NG + g + 1)
                    pe.wait_ge(s_h, 1 + L * 12 + (k - 1 if k >= 2 else 0))
                    mm(PA[0:w, b, :], W1[:, HID + lo:HID + lo + w], xc_group(g), start=True, stop=True)
                    mm(PA[0:w, b + 1, :], W1[:, lo:lo + w], xc_group(g), start=True, stop=True).then_inc(s_f1, 1)
                    if k >= 2:
                        down(k - 2)
                down(3 * NG - 2)
                down(3 * NG - 1)

            def stack(s):
                stack_now[0] = s
                ln_pe(pe, 0 if s == 0 else 8, x_group)
                with pe.Fori(0, DEPTH) as l:
                    L = l + s * DEPTH
                    with pe.Fori(0, NG) as g:
                        attn_group(L * NG + g, g, L)
                    ffn(L)

            pe.wait_ge(s_c_in, 16 * 10)
            pe.wait_ge(s_x_in, 16)
            for t in range(NT):
                last = nc.tensor.transpose(PA[:, t // 4, (t % 4) * P:(t % 4 + 1) * P], XNAT[:, t, :], IDF)
            last.then_inc(s_xt_ps, 1)
            pe.wait_ge(s_xt, 1)
            pe.wait_ge(s_no, 1)
            pe.wait_ge(s_cst, 8)
            stack(0)
            pe.wait_ge(s_xs, NG)
            ln_pe(pe, 7, x_group)
            pe.wait_ge(s_ret_in, 64)
            pe.wait_ge(s_xc, 8 * NG)
            for k in range(4):
                last = nc.tensor.transpose(PA[:, 0, k * P:(k + 1) * P], RW[:, k, :], IDF)
            last.then_inc(s_rwt, 1)
            pe.wait_ge(s_rwe, 1)
            pe.wait_ge(s_lrs, 8 * NG)
            pe.wait_ge(s_rss, 1)
            with pe.Fori(0, NG) as r:
                pe.wait_ge(s_zg, r + 1)
                pe.wait_ge(s_yt, 1 + r * 4)
                mm(PA[:, 0, :], RWT[:, 0, :], ZG, start=True, stop=True)
                mm(PA[:, 1, :], RWT[:, 1, :], ZG, start=True, stop=True).then_inc(s_rq, 1)
                pe.wait_ge(s_rkve, 1 + r)
                for c in range(4):
                    last = mm(PA[:, 2 + c // 2, (c % 2) * 256:(c % 2) * 256 + 256], ZG[:, c * P:(c + 1) * P],
                              RWT[:, 1:3, :], start=True, stop=True)
                last.then_inc(s_rkv, 1)
                pe.wait_ge(s_rqe, 2 * (r + 1))
                for c in range(4):
                    n = r * 4 + c
                    pe.wait_ge(s_qm, n + 1)
                    pe.wait_ge(s_am, 1 + n)
                    for b in range(2):
                        last = mm(PB[:, b, :].rearrange("p (h k) -> p h k", k=P), KR[:, c * P:(c + 1) * P],
                                  QM[:, 4 * b:4 * b + 4, :], start=True, stop=True)
                    last.then_inc(s_ra, 1)
                    if c == 0:
                        pe.wait_ge(s_rqd, r + 1)
                        pe.wait_ge(s_rkd, r + 1)
                    pe.wait_ge(s_rsb, 1 + n)
                    pe.wait_ge(s_yn, 1 + n)
                    mm(PB[:, 2, 0:P], QD[:, c * P:(c + 1) * P], SB, start=True, stop=False, skip_group_check=True)
                    pe.wait_ge(s_am, 1 + n + 1)
                    for h in range(RH):
                        last = mm(PB[:, 2, h * RD:(h + 1) * RD], AM[:, h // 4, (h % 4) * P:(h % 4 + 1) * P],
                                  KV[:, c, P + h * RD:P + (h + 1) * RD], start=False, stop=(h == RH - 1),
                                  skip_group_check=True)
                    last.then_inc(s_ry, 1)
                    mm(PB[:, 3, 0:P], KD[:, c, :], KV[:, c, P:2 * P], start=True, stop=True).then_inc(s_ru, 1)
                    pe.wait_ge(s_yn, 1 + n + 1)
                    nc.tensor.transpose(PA[:, 0, 0:P], YN, IDF).then_inc(s_rtr, 1)
            pe.wait_ge(s_gs1, 1)
            mm(PB[:, 0, 0:1], B16, RST[:, 0:1], start=True, stop=True).then_inc(s_gs1p, 1)
            pe.wait_ge(s_gs2, 1)
            mm(PB[:, 1, 0:1], B16, RST[:, 5:6], start=True, stop=True).then_inc(s_gs2p, 1)
            for g in range(NG):
                pe.wait_ge(s_gy, g + 1)
                mm(PA[:, g, :], RWT[:, 3, :], Y2[:, 1 + g * GT:1 + (g + 1) * GT], start=True, stop=True)\
                    .then_inc(s_ro, 1)
            pe.wait_ge(s_rox, NG)
            stack(1)
            pe.wait_ge(s_xs, 2 * NG)
            for t in range(NT):
                last = nc.tensor.transpose(PA[:, t // 4, (t % 4) * P:(t % 4 + 1) * P], X[:, t * P:(t + 1) * P], IDF)
            last.then_inc(s_fin_ps, 1)


def shape_constants():
    import numpy as np
    f32 = np.float32
    half = np.arange(0, DHEAD, 2, dtype=f32)
    inv_freq = f32(1.0) / np.power(f32(10000.0), half / f32(DHEAD), dtype=f32)
    t = np.arange(NTOK, dtype=f32)
    freqs = (t[:, None] * inv_freq[None, :]).astype(f32)
    base = ((half + f32(0.4 * DHEAD)) / f32(1.4 * DHEAD)).astype(f32)
    power = (t - NTOK // 2) / f32(WIN // 2)
    scale = np.power(base[None, :], power[:, None], dtype=f32)
    cos, sin = np.cos(freqs.astype(np.float64)), np.sin(freqs.astype(np.float64))
    s64 = scale.astype(np.float64)
    ch = np.arange(P) % DHEAD
    d, sign = ch % 32, np.where(ch < 32, -1.0, 1.0)[:, None]
    tables = np.stack([(cos * s64).T[d], (sin * s64).T[d] * sign,
                       (cos / s64).T[d], (sin / s64).T[d] * sign], axis=1).astype(f32)
    norm_in = np.zeros((P, 4, 32), f32)
    norm_out = np.zeros((P, 2 * CH, P), f32)
    for p in range(2 * CH):
        for e in range(2):
            for part in (0, 8):
                norm_in[64 * e:64 * e + 64, p // 4, part + 2 * (p // 4) + e] = 1.0
                norm_out[32 * (p % 4) + part + 2 * (p // 4) + e, p, 64 * e:64 * e + 64] = 1.0
    eye = np.eye(P, dtype=f32)
    blk = (np.arange(P)[:, None] // RD == np.arange(P)[None, :] // RD).astype(f32)
    consts = np.stack([eye, np.full((P, P), 1.0 / P, f32), blk / RD, blk], axis=1).astype(f32)
    big = -1e30
    q = np.arange(P)
    wq, rq = q // WIN, q % WIN
    mask_n = np.zeros((P, 1 + NG, 2 * WIN), f32)
    prev_ok = rq[:, None] <= np.arange(WIN)[None, :]
    own_ok = rq[:, None] >= np.arange(WIN)[None, :]
    mask_n[:, :, 0:WIN] = np.where(prev_ok, 0, big)[:, None, :]
    mask_n[:, :, WIN:] = np.where(own_ok, 0, big)[:, None, :]
    mask_n[0:WIN, 0, 0:WIN] = big
    mask_t = np.full((P, 1 + NG, KCOLS), big, f32)
    dist = q[None, :] - q[:, None]
    ok = (dist >= 0) & (dist <= WIN) & (wq[None, :] - wq[:, None] <= 1)
    mask_t[:, :, 0:P][np.broadcast_to(ok[:, None, :], (P, 1 + NG, P))] = 0
    dist = np.arange(WIN)[None, :] + P - q[:, None]
    ok = (wq[:, None] == 3) & (dist <= WIN)
    mask_t[:, 1:, P:][np.broadcast_to(ok[:, None, :], (P, NG, WIN))] = 0
    sel = np.zeros((P, HEADS + 1, P), f32)
    for h in range(HEADS):
        sel[h, h, :] = 1.0
        sel[HEADS + h, h, :] = 1.0
    sel[:, HEADS, :] = eye
    sgn = np.stack([np.where(q % 32 < 8, 1.0, -1.0), np.where(q % 32 < 8, 0.0, 1.0)], axis=1).astype(f32)
    gam = (f32(1.0) - np.exp(np.linspace(np.log(1.0 / 32.0), np.log(1.0 / 512.0), RH)).astype(f32)).astype(np.float64)
    i = np.arange(P)
    dd = i[None, :] - i[:, None]
    dec_a = np.stack([np.where(dd >= 0, g ** np.maximum(dd, 0), 0.0) for g in gam], axis=1).astype(f32)
    gch = gam[i // RD]
    dq = gch[:, None] ** (i[None, :] + 1)
    dk = gch[None, :] ** (P - 1 - i[:, None])
    hm = np.repeat((np.arange(P)[:, None] // RD == np.arange(RH)[None, :]).astype(f32)[:, :, None], P, axis=2)
    dec_v = np.concatenate([dq[:, None, :], dk[:, None, :], hm], axis=1).astype(f32)
    return tables, norm_in, norm_out, consts, mask_n, mask_t, sel, sgn, dec_a, dec_v, (gch ** P).astype(f32)


def kernel(**inputs):
    import numpy as np
    import ml_dtypes
    import concourse.bacc as bacc
    from concourse import mybir as mb
    from concourse.bass_utils import run_bass_kernel_spmd as run

    a = {k: np.ascontiguousarray(v) for k, v in inputs.items()}
    tables, norm_in, norm_out, consts, mask_n, mask_t, sel, sgn, dec_a, dec_v, gch = shape_constants()
    bf = ml_dtypes.bfloat16
    wqkv = a["L0_ffn_Wqkv"]
    qk = wqkv[:, :, 0:2 * INNER].reshape(DEPTH, P, 2 * HEADS, 2, DHEAD // 2)
    w_attn = np.concatenate([wqkv[:, :, 0:2 * INNER], qk[:, :, :, ::-1].reshape(DEPTH, P, 2 * INNER),
                             wqkv[:, :, 2 * INNER:]], axis=2)
    w_out = a["L0_ffn_Wo"].reshape(DEPTH, CH, P, P).transpose(0, 2, 1, 3).reshape(DEPTH, P, CH * P)
    qs, ks = a["L0_ffn_q_scale"], a["L0_ffn_k_scale"]
    two = lambda v: np.concatenate([v, v], axis=1)
    swap = lambda v: np.concatenate([v[:, DHEAD // 2:], v[:, :DHEAD // 2]], axis=1)
    prm_attn = np.stack([two(qs), two(swap(qs)), two(ks), two(swap(ks))], axis=2)
    pad = 3 * P - HID
    b1 = a["L0_ffn_b1"]
    cols = lambda v: np.concatenate([v, np.zeros((DEPTH, pad), v.dtype)], axis=1).reshape(DEPTH, 3, P).transpose(0, 2, 1)
    prm_ffn = np.concatenate([a["L0_ffn_ln_g"][:, :, None], a["L0_ffn_ln_b"][:, :, None], cols(b1[:, :HID]),
                              cols(b1[:, HID:]), a["L0_ffn_b2"][:, :, None]], axis=2)
    w2 = np.concatenate([a["L0_ffn_W2"], np.zeros((DEPTH, pad, P), np.float32)], axis=1)
    w2 = w2.reshape(DEPTH, 3, P, P).transpose(0, 2, 1, 3).reshape(DEPTH, P, 3 * P)
    w_ret = np.stack([a["L0_attn_Wq"], a["L0_attn_Wk"], a["L0_attn_Wv"], a["L0_attn_Wo"]], axis=1)
    gn = np.stack([a["L0_attn_gn_weight"], a["L0_attn_gn_bias"], gch], axis=1)
    arrays = dict(x=a["L0_attn_x"], w_attn=w_attn, w_out=w_out, prm_attn=prm_attn, w1=a["L0_ffn_W1"], w2=w2,
                  prm_ffn=prm_ffn, w_ret=w_ret, gn=gn, tables=tables, norm_in=norm_in, norm_out=norm_out,
                  consts=consts, mask_n=mask_n.astype(bf), mask_t=mask_t.astype(bf), sel=sel.astype(bf), sgn=sgn,
                  dec_a=dec_a, dec_v=dec_v)
    arrays = {k: np.ascontiguousarray(v) for k, v in arrays.items()}
    nc = bacc.Bacc("TRN2", target_bir_lowering=False, num_devices=1)
    aps = {k: nc.dram_tensor("in_" + k, v.shape, mb.dt.from_np(v.dtype), kind="ExternalInput").ap()
           for k, v in arrays.items()}
    out = nc.dram_tensor("out_0", (1, NTOK, P), mb.dt.float32, kind="ExternalOutput").ap()
    build_macaron(nc, out=out, **aps)
    r = run(nc, [{"in_" + k: v for k, v in arrays.items()}], core_ids=[0])
    return r.results[0]["out_0"]
```
